# Optimizing a Trainium2 kernel written in Bass

```python
import numpy as np
import jax
import jax.numpy as jnp

def _softmax(x, axis=-1):
    return jax.nn.softmax(x, axis=axis)

def _gelu(x):
    return jax.nn.gelu(x, approximate=True)

def _silu(x):
    return jax.nn.silu(x)

def _sigmoid(x):
    return jax.nn.sigmoid(x)

def _layernorm(x, axis=-1, eps=1e-05):
    m = jnp.mean(x, axis=axis, keepdims=True)
    v = jnp.var(x, axis=axis, keepdims=True)
    return (x - m) / jnp.sqrt(v + eps)

def _scatter_add(tgt, idx, src, axis=0):
    return tgt.at[idx].add(src)

def _segment_sum(src, seg, n):
    return jax.ops.segment_sum(src, seg, n)
kernel_name = 'mk_conv_attn_hybrid_d2_conv_nhwc256_r4_900e4d'

def setup_inputs(seed: int=0):
    np.random.seed(seed)
    _w = jnp.asarray

    def _rec_inputs():
        import jax
        import jax.numpy as jnp
        _gk = jax.random.key(seed)
        x = -8.268e-05 + 0.9999 * jax.random.normal(jax.random.fold_in(_gk, 1), (16, 56, 56, 64), jnp.float32)
        return x
    x = _rec_inputs()

    def _L0_conv_setup():
        import jax, jax.numpy as jnp
        import numpy as np
        EPS = 1e-05
        M_PER_GROUP = 16
        ITER_NUM = 5

        def _iter_norm_whiten(x, gamma, beta):
            B, H, W, C = x.shape
            g = C // M_PER_GROUP
            m = M_PER_GROUP
            N = B * H * W
            xt = jnp.transpose(x, (3, 0, 1, 2)).reshape(C, N)
            mu = jnp.mean(xt, axis=1, keepdims=True)
            f = xt - mu
            fg = f.reshape(g, m, N)
            cov = jnp.einsum('gmn,gkn->gmk', fg, fg) / (jnp.float32(N) - 1.0)
            eye = jnp.eye(m, dtype=x.dtype)
            cov = (1.0 - EPS) * cov + EPS * eye
            trace = jnp.trace(cov, axis1=1, axis2=2)[:, None, None]
            sigma = cov / trace
            P = jnp.broadcast_to(eye, (g, m, m))
            for _ in range(ITER_NUM):
                P = (3.0 * P - P @ P @ P @ sigma) / 2.0
            wm = P / jnp.sqrt(trace)
            f_hat = jnp.einsum('gmk,gkn->gmn', wm, fg).reshape(C, B, H, W)
            out = jnp.transpose(f_hat, (1, 2, 3, 0))
            return gamma * out + beta
        key = jax.random.key(seed)
        k1, = jax.random.split(key, 1)
        x = jax.random.normal(k1, (16, 56, 56, 64), dtype=jnp.float32)
        gamma = jnp.ones((1, 1, 1, 64), dtype=jnp.float32)
        beta = jnp.zeros((1, 1, 1, 64), dtype=jnp.float32)
        return {'x': x, 'gamma': gamma, 'beta': beta}
    _L0_conv_all = _L0_conv_setup()
    _L0_conv_in = {k: v for k, v in _L0_conv_all.items() if k in ('gamma', 'beta')}
    del _L0_conv_all

    def _L1_attn_setup():
        import jax, jax.numpy as jnp
        import numpy as np
        WINDOW = 16
        EPS = 1e-05
        key = jax.random.key(seed)
        k1, = jax.random.split(key, 1)
        x = jax.random.normal(k1, (2, 4096, 64), dtype=jnp.float32)
        gamma = jnp.ones((64,), dtype=jnp.float32)
        beta = jnp.zeros((64,), dtype=jnp.float32)
        return {'x': x, 'gamma': gamma, 'beta': beta}
    _L1_attn_all = _L1_attn_setup()
    _L1_attn_in = {k: v for k, v in _L1_attn_all.items() if k in ('gamma', 'beta')}
    del _L1_attn_all

    def _L1_ffn_setup():
        import jax, jax.numpy as jnp
        import numpy as np
        NUM_EXPERTS = 8
        TOP_K = 2
        B, S, D = (8, 2048, 64)

        def _moe(tokens, router_w, w1, b1, w2, b2):
            N = tokens.shape[0]
            E = router_w.shape[0]
            logits = tokens.astype(jnp.float32) @ router_w.astype(jnp.float32).T
            probs = jax.nn.softmax(logits, axis=-1)
            rw, re = jax.lax.top_k(probs, TOP_K)
            if TOP_K > 1:
                rw = rw / jnp.maximum(rw.sum(-1, keepdims=True), 1e-12)
            rw = rw.astype(tokens.dtype)
            combine = jnp.zeros((N, E), tokens.dtype).at[jnp.arange(N)[:, None], re].set(rw)
            out = tokens
            for e in range(E):
                h = jax.nn.gelu(tokens @ w1[e] + b1[e], approximate=False)
                y = h @ w2[e] + b2[e]
                out = out + combine[:, e:e + 1] * y
            return out
        key = jax.random.key(seed)
        ks = jax.random.split(key, 4)
        scale = 1.0 / np.sqrt(D).astype(np.float32)
        return {'input_embeddings': jax.random.normal(ks[0], (B, S, D), jnp.float32), 'router_w': jax.random.normal(ks[1], (NUM_EXPERTS, D), jnp.float32) * scale, 'w1': jax.random.normal(ks[2], (NUM_EXPERTS, D, D), jnp.float32) * scale, 'b1': jnp.zeros((NUM_EXPERTS, D), jnp.float32), 'w2': jax.random.normal(ks[3], (NUM_EXPERTS, D, D), jnp.float32) * scale, 'b2': jnp.zeros((NUM_EXPERTS, D), jnp.float32)}
    _L1_ffn_all = _L1_ffn_setup()
    _L1_ffn_in = {k: v for k, v in _L1_ffn_all.items() if k in ('router_w', 'w1', 'b1', 'w2', 'b2')}
    del _L1_ffn_all
    return {'x': x, 'L0_conv_gamma': _L0_conv_in['gamma'], 'L0_conv_beta': _L0_conv_in['beta'], 'L1_attn_gamma': _L1_attn_in['gamma'], 'L1_attn_beta': _L1_attn_in['beta'], 'L1_ffn_router_w': _L1_ffn_in['router_w'], 'L1_ffn_w1': _L1_ffn_in['w1'], 'L1_ffn_b1': _L1_ffn_in['b1'], 'L1_ffn_w2': _L1_ffn_in['w2'], 'L1_ffn_b2': _L1_ffn_in['b2']}

def reference(x, L0_conv_gamma, L0_conv_beta, L1_attn_gamma, L1_attn_beta, L1_ffn_router_w, L1_ffn_w1, L1_ffn_b1, L1_ffn_w2, L1_ffn_b2):
    import jax
    import jax.numpy as jnp

    def _L0_conv_ref(x, gamma, beta):
        import jax, jax.numpy as jnp
        import numpy as np
        EPS = 1e-05
        M_PER_GROUP = 16
        ITER_NUM = 5

        def _iter_norm_whiten(x, gamma, beta):
            B, H, W, C = x.shape
            g = C // M_PER_GROUP
            m = M_PER_GROUP
            N = B * H * W
            xt = jnp.transpose(x, (3, 0, 1, 2)).reshape(C, N)
            mu = jnp.mean(xt, axis=1, keepdims=True)
            f = xt - mu
            fg = f.reshape(g, m, N)
            cov = jnp.einsum('gmn,gkn->gmk', fg, fg) / (jnp.float32(N) - 1.0)
            eye = jnp.eye(m, dtype=x.dtype)
            cov = (1.0 - EPS) * cov + EPS * eye
            trace = jnp.trace(cov, axis1=1, axis2=2)[:, None, None]
            sigma = cov / trace
            P = jnp.broadcast_to(eye, (g, m, m))
            for _ in range(ITER_NUM):
                P = (3.0 * P - P @ P @ P @ sigma) / 2.0
            wm = P / jnp.sqrt(trace)
            f_hat = jnp.einsum('gmk,gkn->gmn', wm, fg).reshape(C, B, H, W)
            out = jnp.transpose(f_hat, (1, 2, 3, 0))
            return gamma * out + beta
        return _iter_norm_whiten(x, gamma, beta)

    def _L1_attn_ref(x, gamma, beta):
        import jax, jax.numpy as jnp
        import numpy as np
        WINDOW = 16
        EPS = 1e-05
        B, N, D = x.shape
        w = WINDOW
        W = 2 * w + 1
        scale = D ** (-0.5)
        kv_pad = jnp.pad(x, ((0, 0), (w, w), (0, 0)))
        idx = jnp.arange(N)[:, None] + jnp.arange(W)[None, :]
        windows = kv_pad[:, idx]
        scores = jnp.einsum('bnd,bnwd->bnw', x, windows) * scale
        attn = jax.nn.softmax(scores, axis=-1)
        out = jnp.einsum('bnw,bnwd->bnd', attn, windows)
        mu = jnp.mean(out, axis=-1, keepdims=True)
        var = jnp.var(out, axis=-1, keepdims=True)
        out = (out - mu) * jax.lax.rsqrt(var + EPS) * gamma + beta
        return out

    def _L1_ffn_ref(input_embeddings, router_w, w1, b1, w2, b2):
        import jax, jax.numpy as jnp
        import numpy as np
        NUM_EXPERTS = 8
        TOP_K = 2
        B, S, D = (8, 2048, 64)

        def _moe(tokens, router_w, w1, b1, w2, b2):
            N = tokens.shape[0]
            E = router_w.shape[0]
            logits = tokens.astype(jnp.float32) @ router_w.astype(jnp.float32).T
            probs = jax.nn.softmax(logits, axis=-1)
            rw, re = jax.lax.top_k(probs, TOP_K)
            if TOP_K > 1:
                rw = rw / jnp.maximum(rw.sum(-1, keepdims=True), 1e-12)
            rw = rw.astype(tokens.dtype)
            combine = jnp.zeros((N, E), tokens.dtype).at[jnp.arange(N)[:, None], re].set(rw)
            out = tokens
            for e in range(E):
                h = jax.nn.gelu(tokens @ w1[e] + b1[e], approximate=False)
                y = h @ w2[e] + b2[e]
                out = out + combine[:, e:e + 1] * y
            return out
        b, s, d = input_embeddings.shape
        tokens = input_embeddings.reshape(b * s, d)
        return _moe(tokens, router_w, w1, b1, w2, b2).reshape(b, s, d)

    def _gn(v, G=32, eps=1e-05):
        B_, H_, W_, C_ = v.shape
        g = v.reshape(B_, H_, W_, G, C_ // G)
        m = jnp.mean(g, axis=(1, 2, 4), keepdims=True)
        s = jnp.var(g, axis=(1, 2, 4), keepdims=True)
        return ((g - m) / jnp.sqrt(s + eps)).reshape(v.shape)

    def _ln_c(v, eps=1e-06):
        m = jnp.mean(v, axis=-1, keepdims=True)
        s = jnp.var(v, axis=-1, keepdims=True)
        return (v - m) / jnp.sqrt(s + eps)

    def _ln_t(v, eps=1e-05):
        m = jnp.mean(v, axis=-1, keepdims=True)
        s = jnp.var(v, axis=-1, keepdims=True)
        return (v - m) / jnp.sqrt(s + eps)

    def _to_tokens(v):
        B_, H_, W_, C_ = v.shape
        return v.reshape(B_, H_ * W_, C_)

    def _from_tokens(t, like):
        return t.reshape(like.shape)
    x = _L0_conv_ref(x, L0_conv_gamma, L0_conv_beta)
    t = _to_tokens(x)
    t = t + _L1_attn_ref(_ln_t(t), L1_attn_gamma, L1_attn_beta)
    t = t + _L1_ffn_ref(_ln_t(t), L1_ffn_router_w, L1_ffn_w1, L1_ffn_b1, L1_ffn_w2, L1_ffn_b2)
    x = _from_tokens(t, x)
    return x

_drawn_inputs = setup_inputs


def setup_inputs(seed=0):
    import zlib

    import numpy as np

    out = dict(_drawn_inputs(seed))
    spreads = {'L0_conv_gamma': (1.0, 0.2),
     'L0_conv_beta': (0.0, 0.1),
     'L1_attn_gamma': (1.0, 0.2),
     'L1_attn_beta': (0.0, 0.1),
     'L1_ffn_b1': (0.0, 0.505),
     'L1_ffn_b2': (0.0, 0.322)}
    factors = {}
    for name, (base, spread) in spreads.items():
        noise = np.random.default_rng([zlib.crc32(name.encode()), seed]).standard_normal(out[name].shape)
        drawn = base * np.exp(spread * noise) if base else spread * noise
        out[name] = jnp.asarray(drawn.astype(out[name].dtype))
    for name, factor in factors.items():
        out[name] = (out[name] * factor).astype(out[name].dtype)
    return out
```

```python
import concourse.bass as bass
from concourse import mybir
from contextlib import ExitStack

H = 2
BLK = 64
NB = 7
CH = NB * BLK
C = 64
WIN = 16
KEYS = BLK + 2 * WIN
E = 8
PARTS = 3
CP = 32
M_GROUP = 16
ITERS = 5
EPS_W = 1e-5
EPS_LN = 1e-5
SLOT2 = [0, 1, 0, 1, 0, 1, 2]
SLOT3 = [0, 1, 2, 0, 1, 2, 3]


def hybrid_kernel(nc, x, g0, b0, g1, b1v, rw, w1, b1, w2, b2, k_eye, k_fold, k_group, k_block, k_band,
                  k_rank, k_sel, out):
    f32, bf16, f32r = mybir.dt.float32, mybir.dt.bfloat16, mybir.dt.float32r
    ALU, ACT, AX = mybir.AluOpType, mybir.ActivationFunctionType, mybir.AxisListType
    IMGS, HH, WW, _ = x.shape
    NP = IMGS // H
    TOK = HH * WW
    CPI = TOK // CH
    G = NP * CPI
    N = IMGS * TOK
    PTOK = H * TOK // 128
    assert CPI == 7 and G % 2 == 0 and PTOK * 128 == H * TOK
    SCALE = float(C) ** -0.5

    x_flat = x.rearrange("i a b c -> (i a b c)")
    x_pairs = x_flat.rearrange("(n p f) -> n p f", n=NP, p=128)
    x_chunks = x_flat.rearrange("(h g b p c) -> h g p b c", h=H, g=G, b=NB, p=BLK)
    out_chunks = out.rearrange("i a b c -> (i a b c)").rearrange("(h g b p c) -> h g p b c", h=H, g=G, b=NB, p=BLK)
    spill = nc.dram_tensor("tn_spill", (G, 128, CH), f32).ap()

    ctx = ExitStack()
    with ctx:
        def sb(name, shape, dt=f32):
            return ctx.enter_context(nc.sbuf_tensor(name, shape, dt))

        def pb(name, shape):
            return ctx.enter_context(nc.psum_tensor(name, shape, f32))

        def sem(name):
            return ctx.enter_context(nc.semaphore(name))

        resid = sb("resid", [128, G * CH])
        comb = sb("comb", [128, G * NB * E])
        eye = sb("eye", [128, 128])
        band = sb("band", [KEYS, BLK])
        rank = sb("rank", [128, E])
        selector = sb("selector", [128, H * 4 * 128], bf16)
        eye_h = sb("eye_h", [128, 128], bf16)
        bet0 = sb("bet0", [128, C])
        gam1 = sb("gam1", [128, C])
        bet1 = sb("bet1", [128, C])
        white = sb("white", [128, H, C])
        router = sb("router", [128, H, E])
        neg_mean = sb("neg_mean", [128, 1])
        w1_hi = sb("w1_hi", [128, E * C], f32r)
        w1_lo = sb("w1_lo", [128, E * C], f32r)
        w2_s = sb("w2_s", [128, 4, C])
        b1_s = sb("b1_s", [128, 4])
        b2_p = sb("b2_p", [128, PARTS, H * C], bf16)
        ARENA = 9840
        arena = sb("arena", [128, ARENA])
        logits = sb("logits", [128, NB * CPI, E])

        def carve(at, shape, dt=f32, rows=128):
            n = 1
            for s in shape:
                n *= s
            assert at[0] + (n if dt != bf16 else n // 2) <= ARENA, (at, n)
            view = arena[0:rows, at[0]:at[0] + (n if dt != bf16 else (n + 1) // 2)]
            at[0] += n if dt != bf16 else (n + 1) // 2
            if dt != f32:
                view = view.bitcast(dt)
            if len(shape) == 2:
                view = view.rearrange("p (a b) -> p a b", a=shape[0])
            if len(shape) == 3:
                view = view.rearrange("p (a b c) -> p a b c", a=shape[0], b=shape[1])
            return view

        at = [0]
        x1 = carve(at, [2, PTOK * C])
        colsum = carve(at, [NP, C])
        colsum2 = carve(at, [2, C])
        gram = carve(at, [C])
        srow = carve(at, [C])
        scol = carve(at, [1])
        outer = carve(at, [C])
        psig = carve(at, [2, C])
        pq = carve(at, [2, C])
        p15 = carve(at, [C])
        covd = carve(at, [C])
        small1 = carve(at, [16])
        rmat = carve(at, [C])
        sel_f = carve(at, [H * 4 * 128])
        w1_f = carve(at, [E * C])
        b2_f = carve(at, [H * C])
        fold = carve(at, [128])
        ones = carve(at, [128])
        group = carve(at, [64], rows=64)
        block = carve(at, [64])
        gam0 = carve(at, [C], rows=64)
        at = [0]
        x2 = carve(at, [4, CH])
        keys_t = carve(at, [7, CH + 2 * WIN])
        qry = [carve(at, [3, CH]) for _ in range(H)]
        pick = carve(at, [3, NB * CPI * E]).rearrange("p k (t e) -> p k t e", e=E)
        at3 = [0]
        tdup = carve(at3, [2, H * CH])
        hid = carve(at3, [2, H * CH])
        gated = carve(at3, [2, H * CH])
        y3 = carve(at3, [CH])
        fin = carve(at3, [2, CH])
        ct_s = carve(at3, [2, CH], bf16)
        cf = carve(at3, [NB, E])
        cr = carve(at3, [NB, E])
        cparts = carve(at3, [2, NB * CP], bf16)

        with nc.sbuf_tensor("yb", [128, 7, CH], f32) as yb:
            pass
        thl = sb("thl", [128, 2, H, CH], f32r)
        sb("rest_of_yb", [128, 7 * CH - 2 * H * CH])
        xt_s = sb("xt_s", [128, CH])
        y_s = sb("y_s", [128, NB, C])
        xn_s = sb("xn_s", [128, NB, C])
        v_s = sb("v_s", [KEYS, NB, H, C + 1])
        prob = sb("prob", [KEYS, H, CH])
        sq = sb("sq", [128, NB, C + 1])
        t_s = sb("t_s", [128, 3, NB, C])
        tn_s = sb("tn_s", [128, 3, NB, C])
        tnt_s = sb("tnt_s", [128, 3, CH])
        st1, st3 = sb("st1", [128, NB, 6]), sb("st3", [128, NB, 6])
        sm = sb("sm", [128, 3, 12, NB])
        top = sb("top", [128, 5, NB * CPI])

        p01 = pb("p01", [128, 2, 512])
        p2 = pb("p2", [128, 512])
        p34 = pb("p34", [128, 2, 512])
        p56 = pb("p56", [128, 2, 512])
        p7 = pb("p7", [128, 512])

        s_const, s_weights, s_x1 = sem("consts_in"), sem("weights_in"), [sem(f"x1_in{i}") for i in range(2)]
        s_zero, s_prep, s_prep_pool = sem("zeroed"), sem("prep_done"), sem("prep_pool")
        s_gram, s_colsum = sem("gram_done"), sem("colsum_done")
        s_cd, s_cp, s_ca = sem("chain_dve"), sem("chain_pe"), sem("chain_act")
        s_x2 = [sem(f"x2_in{i}") for i in range(7)]
        s_xt, s_xts, s_y, s_ys, s_yb = sem("xt"), sem("xt_copied"), sem("y"), sem("y_copied"), sem("yb")
        s_v1, s_w1, s_r1, s_n1, s_xn = sem("ln1_steps"), sem("ln1_var"), sem("ln1_rsqrt"), sem("ln1_newton"), sem("xn")
        s_xnt, s_xnts = sem("xn_t"), sem("xn_t_copied")
        s_v, s_vs, s_s, s_p, s_pm, s_o = sem("v"), sem("v_copied"), sem("scores"), sem("probs"), sem("probs_masked"), sem("pv")
        s_sq, s_v2, s_w2, s_r2, s_n2, s_t = sem("pv_squared"), sem("ln2_steps"), sem("ln2_var"), sem("ln2_rsqrt"), sem("ln2_newton"), sem("t_scaled")
        s_tp, s_t2 = sem("t_gamma"), sem("t2")
        s_v3, s_w3, s_r3, s_n3, s_tn = sem("ln3_steps"), sem("ln3_var"), sem("ln3_rsqrt"), sem("ln3_newton"), sem("tn")
        s_ra = [sem(f"act_ln{i}") for i in range(3)]
        s_res, s_tnt, s_tnts, s_l, s_ls = sem("resid"), sem("tn_t"), sem("tn_t_copied"), sem("logits"), sem("logits_copied")
        s_sp = [sem(f"spilled{i}") for i in range(3)]
        s_top, s_gap, s_gexp, s_comb = sem("top_steps"), sem("top_gap"), sem("top_exp"), sem("combined")
        s_comb2 = sem("combine_steps")
        s_td = [sem(f"tdup_in{i}") for i in range(2)]
        s_hi, s_lo, s_cs, s_cpt = sem("tn_hi"), sem("tn_lo"), sem("comb_steps"), sem("comb_parts")
        s_ct, s_cts = sem("comb_t"), sem("comb_t_copied")
        s_h, s_g, s_c, s_gm = sem("hidden"), sem("gelu"), sem("weights_spread"), sem("gated")
        s_l2, s_y3s, s_tt, s_fin = sem("second_layer"), sem("expert_sum_copied"), sem("back_t"), sem("fin")
        s_out = [sem(f"stored{i}") for i in range(2)]

        def wait(eng, s, n):
            if not isinstance(n, int) or n > 0:
                eng.wait_ge(s, n)

        def walk(eng, step, period, chunks, skew):
            assert chunks % period == 0 and skew <= period
            for c in range(period):
                step(c, c, lambda d, c=c: d <= c)
            with eng.Fori(1, chunks // period) as i:
                for c in range(period):
                    step(i * period + c, c, lambda d: True)
            for c in range(skew):
                step(chunks + c, c, lambda d, c=c: d > c)

        def prv(c, d, n=7):
            return (c - d) % n

        blk = ctx.enter_context(nc.Block())

        @blk.sync
        def _(sp):
            sp.dma_start(x1[:, 0, :], x_pairs[0]).then_inc(s_x1[0], 16)
            sp.dma_start(x1[:, 1, :], x_pairs[1]).then_inc(s_x1[1], 16)
            for dst, src in ((eye[:, :], k_eye), (fold, k_fold), (group, k_group),
                             (block, k_block), (band[:, :], k_band),
                             (rank[:, :], k_rank.partition_broadcast(128)), (sel_f[:, :], k_sel),
                             (gam0, g0.rearrange("a b c d -> (a b c d)").partition_broadcast(64)),
                             (bet0[:, :], b0.rearrange("a b c d -> (a b c d)").partition_broadcast(128)),
                             (gam1[:, :], g1.partition_broadcast(128)),
                             (bet1[:, :], b1v.partition_broadcast(128))):
                sp.dma_start(dst, src).then_inc(s_const, 16)
            with sp.Fori(1, NP // 2) as i:
                for k in range(2):
                    n = i * 2
                    sp.wait_ge(s_gram, n + k - 1)
                    sp.wait_ge(s_colsum, n + k - 1)
                    sp.dma_start(x1[:, k, :], x_pairs[n + k]).then_inc(s_x1[k], 16)
            sp.wait_ge(s_prep, 1)

            def step(g, c, has):
                if has(0):
                    wait(sp, s_xt, g - 2)
                    for h in range(H):
                        sp.dma_start(x2[64 * h:64 * h + 64, SLOT3[c], :].rearrange("p (b c) -> p b c", b=NB),
                                     x_chunks[h, g]).then_inc(s_x2[c], 16)

            walk(sp, step, 7, G, 0)

            sp.wait_ge(s_s, G)
            sp.wait_ge(s_comb, NP)
            for k in range(3):
                spilled = sum(1 for c in range(7) if SLOT2[c] == k) * NP
                sp.wait_ge(s_sp[k], 16 * spilled)

            def step3(g, c, has):
                if has(0):
                    wait(sp, s_hi, g - 1)
                    wait(sp, s_lo, g - 1)
                    for d in range(2):
                        sp.dma_start(tdup[64 * d:64 * d + 64, c, :].rearrange("p (h n) -> p h n", h=H),
                                     spill[g].rearrange("(h p) n -> p h n", h=H)).then_inc(s_td[c], 16)
                if has(2):
                    wait(sp, s_fin, g - 1)
                    for h in range(H):
                        sp.dma_start(out_chunks[h, g - 2], fin[64 * h:64 * h + 64, c, :].rearrange("p (b c) -> p b c", b=NB))\
                          .then_inc(s_out[c], 16)

            walk(sp, step3, 2, G, 2)
            for c in range(2):
                sp.wait_ge(s_out[c], 32 * (G // 2))

        @blk.gpsimd
        def _(pool):
            v = nc.gpsimd
            for dst, src in ((w1_f[0:64, :].rearrange("d (e f) -> d e f", e=E), w1.rearrange("e d f -> d e f")),
                             (w1_f[64:128, :].rearrange("d (e f) -> d e f", e=E), w1.rearrange("e d f -> d e f")),
                             (w2_s[:, :, :], w2.rearrange("(j e) f d -> (e f) j d", e=2)),
                             (b1_s[:, :], b1.rearrange("(j e) f -> (e f) j", e=2))):
                pool.dma_start(dst, src, allow_slow_non_contiguous=True).then_inc(s_weights, 16)
            v.memset(router[:, :, :], 0.0)
            v.memset(b2_f[:, :], 0.0)
            v.memset(white[:, :, :], 0.0)
            v.memset(ones, 1.0)
            v.memset(v_s[:, :, :, :], 1.0).then_inc(s_zero, 1)
            pool.wait_ge(s_zero, 1)
            for h in range(H):
                pool.dma_start(router[64 * h:64 * h + 64, h, :], rw.rearrange("e c -> c e"),
                               allow_slow_non_contiguous=True).then_inc(s_weights, 16)
                for p in range(PARTS):
                    r = CP * h + E * p
                    pool.dma_start(b2_f[r:r + E, C * h:C * h + C], b2).then_inc(s_weights, 16)
            pool.wait_ge(s_weights, 16 * (4 + H * (1 + PARTS)))
            pool.wait_ge(s_const, 16 * 11)
            n = 0
            v.tensor_copy(selector[:, :], sel_f)
            v.tensor_copy(eye_h[:, :], eye[:, :])
            for p in range(PARTS):
                v.tensor_copy(b2_p[:, p, :], b2_f).then_inc(s_prep_pool, 1)
                n += 1
                pool.wait_ge(s_prep_pool, n)
                if p < PARTS - 1:
                    v.tensor_tensor(b2_f, b2_f, b2_p[:, p, :], ALU.subtract).then_inc(s_prep_pool, 1)
                    n += 1
                    pool.wait_ge(s_prep_pool, n)

            pool.wait_ge(s_prep, 1)
            for h in range(H):
                v.memset(qry[h], 0.0)
            v.memset(keys_t[:, 0, 0:WIN], 0.0)
            v.memset(keys_t[:, 6, WIN + CH:], 0.0).then_inc(s_zero, 1)

            def step(g, c, has):
                if has(4):
                    q, cq = g - 4, prv(c, 4)
                    sl = SLOT2[cq]
                    wait(pool, s_t, q + 1)
                    v.tensor_tensor(t_s[:, sl], t_s[:, sl], gam1[:, :].unsqueeze(1).to_broadcast([128, NB, C]),
                                    ALU.mult).then_inc(s_tp, 1)
                    wait(pool, s_tp, q + 1)
                    v.tensor_tensor(t_s[:, sl], t_s[:, sl], yb[:, cq].rearrange("p (b c) -> p b c", b=NB),
                                    ALU.add).then_inc(s_t2, 1)
                if has(5):
                    wait(pool, s_tn, g - 4)
                if has(0):
                    wait(pool, s_ys, g + 1)
                    v.tensor_tensor(yb[:, c].rearrange("p (b c) -> p b c", b=NB), y_s[:, :, :],
                                    bet1[:, :].unsqueeze(1).to_broadcast([128, NB, C]), ALU.add).then_inc(s_yb, 1)
                if has(5):
                    q, sl = g - 5, SLOT2[prv(c, 5)]
                    v.tensor_tensor(resid[:, bass.ds(q * CH, CH)], t_s[:, sl].rearrange("p b c -> p (b c)"),
                                    tn_s[:, sl].rearrange("p b c -> p (b c)"), ALU.add).then_inc(s_res, 1)
                if has(2):
                    q = g - 2
                    wait(pool, s_p, q + 1)
                    pv = prob[:, :, :].rearrange("p h (b q) -> p (h b) q", b=NB)
                    v.tensor_tensor(pv, pv, band[:, :].unsqueeze(1).to_broadcast([KEYS, H * NB, BLK]),
                                    ALU.mult).then_inc(s_pm, 1)

            walk(pool, step, 7, G, 5)

            pool.wait_ge(s_s, G)
            pool.wait_ge(s_comb, NP)
            v.memset(ct_s, 0.0)
            v.memset(cparts, 0.0).then_inc(s_zero, 1)

        @blk.scalar
        def _(act):
            a = nc.scalar
            a.preload_act_table_set("natural_log_exp_and_others")
            act.wait_ge(s_weights, 16 * (4 + H * (1 + PARTS)))
            a.activation(w1_hi[:, :], w1_f, ACT.Copy).then_inc(s_ca, 1)
            act.wait_ge(s_cd, 10)
            a.activation(small1[0:64, 3:4], small1[0:64, 0:1], ACT.Ln).then_inc(s_ca, 1)
            act.wait_ge(s_ca, 2)
            a.activation(small1[0:64, 4:5], small1[0:64, 3:4], ACT.Exp, scale=-0.5).then_inc(s_ca, 1)

            def rsqrt(k, g, s_w, s_r):
                wait(act, s_w, g + 1)
                a.activation(sm[:, k, 6, :], sm[:, k, 5, :], ACT.Ln).then_inc(s_ra[k], 1)
                wait(act, s_ra[k], g + 1)
                a.activation(sm[:, k, 7, :], sm[:, k, 6, :], ACT.Exp, scale=-0.5).then_inc(s_r, 1)

            act.wait_ge(s_prep, 1)

            def step(g, c, has):
                if has(0):
                    wait(act, s_xt, g + 1)
                    wait(act, s_y, g)
                    a.activation(xt_s[:, :], p01[:, 0, 0:CH], ACT.Identity, bias=neg_mean[:, :]).then_inc(s_xts, 1)
                if has(1):
                    q, cq = g - 1, prv(c, 1)
                    wait(act, s_xnt, q + 1)
                    wait(act, s_s, q - 1)
                    if isinstance(q, int) and q == 0:
                        act.wait_ge(s_zero, 2)
                    for h in range(H):
                        r = slice(64 * h, 64 * h + 64)
                        a.activation(qry[h][r, SLOT2[cq], :], p2[r, 0:CH], ACT.Copy)
                    if cq < 6:
                        a.activation(keys_t[:, cq + 1, 0:WIN], p2[:, CH - WIN:CH], ACT.Copy)
                    if cq > 0:
                        a.activation(keys_t[:, cq - 1, WIN + CH:], p2[:, 0:WIN], ACT.Copy)
                    a.activation(keys_t[:, cq, WIN:WIN + CH], p2[:, 0:CH], ACT.Copy).then_inc(s_xnts, 1)
                if has(3):
                    q = g - 3
                    wait(act, s_o, q + 1)
                    wait(act, s_w2, q)
                    a.activation(sq[:, :, :], p7[:, 0:NB * (C + 1)].rearrange("p (b c) -> p b c", b=NB),
                                 ACT.Square).then_inc(s_sq, 1)
                if has(2):
                    q = g - 2
                    wait(act, s_v, q + 1)
                    wait(act, s_o, q)
                    for k, (lo, n) in enumerate(((0, 4), (4, 3))):
                        last = a.activation(v_s[:, lo:lo + n, :, 0:C],
                                            p56[0:KEYS, k, 0:n * 128].rearrange("p (b h c) -> p b h c", b=n, h=H),
                                            ACT.Copy)
                    last.then_inc(s_vs, 1)
                if has(0):
                    rsqrt(0, g, s_w1, s_r1)
                if has(4):
                    rsqrt(2, g - 4, s_w3, s_r3)
                if has(3):
                    rsqrt(1, g - 3, s_w2, s_r2)
                if has(2):
                    q = g - 2
                    wait(act, s_s, q + 1)
                    a.activation(prob[:, :, :], p34[0:KEYS, :, 0:CH], ACT.Exp, scale=SCALE).then_inc(s_p, 1)
                if has(5):
                    q, sl = g - 5, SLOT2[prv(c, 5)]
                    wait(act, s_tnt, q + 1)
                    wait(act, s_l, q - 1)
                    if not isinstance(q, int) or q >= 2:
                        uses = sum(1 for k in range(prv(c, 5)) if SLOT2[k] == sl)
                        per = sum(1 for k in range(7) if SLOT2[k] == sl)
                        n = (q - prv(c, 5)) // 7 * per + uses if isinstance(q, int) else None
                        if n is None:
                            n = spill_count(q, prv(c, 5), per, uses)
                        wait(act, s_sp[sl], 16 * n)
                    a.activation(tnt_s[:, sl, :], p01[:, 0, 0:CH], ACT.Copy).then_inc(s_tnts, 1)
                    wait(act, s_tnts, q + 1)
                    act.dma_start(spill[q], tnt_s[:, sl, :]).then_inc(s_sp[sl], 16)
                if has(6) and prv(c, 6) == 6:
                    im = (g - 6 - 6) // 7 if isinstance(g, int) else image_of(g, c)
                    wait(act, s_gap, im + 1)
                    a.activation(top[:, 3, :], top[:, 2, :], ACT.Exp).then_inc(s_gexp, 1)

            cur = {}

            def spill_count(q, cq, per, uses):
                return cur["i"](cq) * per + uses

            def image_of(g, c):
                return cur["i"](6)

            def walk_act():
                for g in range(14):
                    step(g, g % 7, lambda d, g=g: d <= g)
                with act.Fori(2, G // 7) as i:
                    for c in range(7):
                        cur["i"] = lambda cq, c=c: i if cq <= c else i - 1
                        step(i * 7 + c, c, lambda d: True)
                for c in range(7):
                    step(G + c, c, lambda d, c=c: d > c)

            walk_act()

            def gelu(g, c, j):
                u = g * 4 + j
                wait(act, s_h, u + 1)
                wait(act, s_gm, u - 1)
                a.activation(hid[:, j % 2, :].rearrange("p (h n) -> p h n", h=H),
                             (p34 if j % 2 == 0 else p56)[:, :, 0:CH], ACT.Gelu, bias=b1_s[:, j:j + 1]).then_inc(s_g, 1)

            def high(g, c):
                if isinstance(g, int) and g >= G:
                    return
                n = cur["round"](g)
                wait(act, s_td[c], 32 * n)
                wait(act, s_h, 4 * (g - 1))
                a.activation(thl[:, c], tdup[:, c].rearrange("p (h n) -> p h n", h=H), ACT.Copy).then_inc(s_hi, 1)

            def step3(g, c, has, i):
                if has(0):
                    gelu(g, c, 0)
                    gelu(g, c, 1)
                if has(1):
                    wait(act, s_l2, 4 * g)
                    wait(act, s_tt, g - 1)
                    a.activation(y3, p2[:, 0:CH], ACT.Copy).then_inc(s_y3s, 1)
                if has(0):
                    gelu(g, c, 2)
                    if not (isinstance(g, int) and g + 1 >= G):
                        cur["round"] = lambda _: (i + 1 if c == 0 else i + 2)
                        high(g + 1, 1 - c)
                    gelu(g, c, 3)

            cur["round"] = lambda _: 1
            act.wait_ge(s_comb, NP)
            high(0, 0)
            step3(0, 0, lambda d: d <= 0, 0)
            step3(1, 1, lambda d: d <= 1, 0)
            with act.Fori(1, G // 2 - 1) as i:
                step3(i * 2, 0, lambda d: True, i)
                step3(i * 2 + 1, 1, lambda d: True, i)
            step3(G - 2, 0, lambda d: True, G // 2 - 1)
            step3(G - 1, 1, lambda d: True, G // 2 - 1)
            step3(G, 0, lambda d: d > 0, G // 2)

        @blk.vector
        def _(dve):
            v = nc.vector
            n_cd = [0]

            def link(ins):
                n_cd[0] += 1
                ins.then_inc(s_cd, 1)
                dve.wait_ge(s_cd, n_cd[0])

            for k in range(2):
                dve.wait_ge(s_x1[k], 16)
                v.tensor_reduce(colsum[:, k, :], x1[:, k, :].rearrange("p (t c) -> p c t", c=C), AX.X, ALU.add).then_inc(s_colsum, 1)
            for n in range(2, NP):
                dve.wait_ge(s_x1[n % 2], 16 * (n // 2 + 1))
                v.tensor_reduce(colsum[:, n, :], x1[:, n % 2, :].rearrange("p (t c) -> p c t", c=C), AX.X, ALU.add).then_inc(s_colsum, 1)
            dve.wait_ge(s_colsum, NP)
            for k in range(2):
                last = v.tensor_reduce(colsum2[:, k, :], colsum.rearrange("p n c -> p c n"), AX.X, ALU.add)
            link(last)
            dve.wait_ge(s_gram, NP)
            link(v.tensor_copy(gram, p34[:, 0, 0:C]))
            dve.wait_ge(s_cp, 1)
            v.tensor_copy(scol, p2[:, C:C + 1])
            link(v.tensor_copy(srow, p2[:, 0:C]))
            v.tensor_scalar(neg_mean[:, :], scol, -1.0 / N, None, ALU.mult)
            link(v.tensor_scalar(outer, srow, scol, -1.0 / N, ALU.mult, ALU.mult))
            link(v.tensor_tensor(outer, outer, p2[:, 2 * C:3 * C], ALU.add))
            link(v.tensor_tensor(outer, outer, block, ALU.mult))
            link(v.scalar_tensor_tensor(covd[0:64], eye[0:64, 0:64], EPS_W, outer[0:64], ALU.mult, ALU.add))
            link(v.tensor_tensor(p15[0:64], covd[0:64], eye[0:64, 0:64], ALU.mult))
            link(v.tensor_reduce(small1[0:64, 1:2], p15[0:64], AX.X, ALU.add))
            dve.wait_ge(s_cp, 2)
            link(v.tensor_copy(small1[0:64, 0:1], p7[0:64, 0:1]))
            link(v.reciprocal(small1[0:64, 2:3], small1[0:64, 0:1]))
            link(v.tensor_scalar(psig[0:64, 1, :], covd[0:64], small1[0:64, 2:3], None, ALU.mult))
            link(v.tensor_scalar(p15[0:64], eye[0:64, 0:64], 1.5, None, ALU.mult))
            link(v.scalar_tensor_tensor(psig[0:64, 0, :], psig[0:64, 1, :], -0.5, p15[0:64], ALU.mult, ALU.add))
            for it in range(ITERS - 1):
                dve.wait_ge(s_cp, 3 + 2 * it)
                v.tensor_scalar(p15[0:64], psig[0:64, 0, :], 1.5, None, ALU.mult)
                link(v.tensor_copy(pq[0:64].rearrange("p a b -> p (a b)"), p2[0:64, 0:2 * C]))
                dve.wait_ge(s_cp, 4 + 2 * it)
                link(v.scalar_tensor_tensor(psig[0:64, 0, :], p7[0:64, 0:C], -0.5, p15[0:64], ALU.mult, ALU.add))
            dve.wait_ge(s_ca, 3)
            link(v.tensor_tensor(small1[0:64, 5:6], small1[0:64, 0:1], small1[0:64, 4:5], ALU.mult))
            link(v.scalar_tensor_tensor(small1[0:64, 6:7], small1[0:64, 5:6], -0.5, small1[0:64, 4:5], ALU.mult, ALU.mult))
            link(v.scalar_tensor_tensor(small1[0:64, 7:8], small1[0:64, 6:7], 1.5, small1[0:64, 4:5], ALU.add, ALU.mult))
            link(v.tensor_scalar(rmat[0:64], psig[0:64, 0, :], small1[0:64, 7:8], None, ALU.mult))
            link(v.tensor_tensor(rmat[0:64], rmat[0:64], gam0, ALU.mult))
            v.tensor_tensor(w1_lo[:, :], w1_f, w1_hi[:, :].bitcast(f32), ALU.subtract)
            dve.wait_ge(s_cp, 3 + 2 * (ITERS - 1))
            dve.wait_ge(s_zero, 1)
            v.tensor_copy(white[0:64, 0, :], p2[0:64, 0:C])
            dve.wait_ge(s_prep_pool, 2 * PARTS - 1)
            v.tensor_copy(white[64:128, 1, :], p2[64:128, 0:C]).then_inc(s_prep, 1)

            def ln_stats(k, g, src, st, s_v, s_w):
                for b in range(NB):
                    last = v.bn_stats(st[:, b, :], src[:, b, :])
                last.then_inc(s_v, 1)
                wait(dve, s_v, g * 4 + 1)
                v.tensor_tensor(sm[:, k, 0, :], st[:, :, 1], st[:, :, 4], ALU.add)
                v.tensor_tensor(sm[:, k, 1, :], st[:, :, 1], st[:, :, 4], ALU.subtract)
                v.tensor_tensor(sm[:, k, 2, :], st[:, :, 2], st[:, :, 5], ALU.add).then_inc(s_v, 1)
                wait(dve, s_v, g * 4 + 2)
                v.tensor_scalar(sm[:, k, 3, :], sm[:, k, 0, :], 0.5, None, ALU.mult)
                v.tensor_tensor(sm[:, k, 4, :], sm[:, k, 1, :], sm[:, k, 1, :], ALU.mult).then_inc(s_v, 1)
                wait(dve, s_v, g * 4 + 3)
                v.scalar_tensor_tensor(sm[:, k, 4, :], sm[:, k, 4, :], C / 4.0, sm[:, k, 2, :], ALU.mult, ALU.add).then_inc(s_v, 1)
                wait(dve, s_v, g * 4 + 4)
                v.tensor_scalar(sm[:, k, 5, :], sm[:, k, 4, :], 1.0 / C, EPS_LN, ALU.mult, ALU.add).then_inc(s_w, 1)

            def newton(k, g, s_r, s_n):
                wait(dve, s_r, g + 1)
                v.tensor_tensor(sm[:, k, 8, :], sm[:, k, 5, :], sm[:, k, 7, :], ALU.mult).then_inc(s_n, 1)
                wait(dve, s_n, g * 3 + 1)
                v.scalar_tensor_tensor(sm[:, k, 9, :], sm[:, k, 8, :], -0.5, sm[:, k, 7, :], ALU.mult, ALU.mult).then_inc(s_n, 1)
                wait(dve, s_n, g * 3 + 2)
                v.scalar_tensor_tensor(sm[:, k, 10, :], sm[:, k, 9, :], 1.5, sm[:, k, 7, :], ALU.add, ALU.mult).then_inc(s_n, 1)
                wait(dve, s_n, g * 3 + 3)

            def step(g, c, has):
                if has(0):
                    wait(dve, s_y, g + 1)
                    wait(dve, s_yb, g)
                    v.tensor_tensor(y_s[:, :, :], p01[:, 1, 0:CH].rearrange("p (b c) -> p b c", b=NB),
                                    bet0[:, :].unsqueeze(1).to_broadcast([128, NB, C]), ALU.add).then_inc(s_ys, 1)
                    wait(dve, s_ys, g + 1)
                    ln_stats(0, g, y_s, st1, s_v1, s_w1)
                if has(4):
                    q, sl = g - 4, SLOT2[prv(c, 4)]
                    wait(dve, s_t2, q + 1)
                    ln_stats(2, q, t_s[:, sl], st3, s_v3, s_w3)
                if has(3):
                    q = g - 3
                    wait(dve, s_sq, q + 1)
                    v.tensor_reduce(sm[:, 1, 0, :], sq[:, :, 0:C], AX.X, ALU.add)
                    v.tensor_scalar(sm[:, 1, 1, :], sq[:, :, C], EPS_LN, None, ALU.mult).then_inc(s_v2, 1)
                    wait(dve, s_v2, q + 1)
                    v.scalar_tensor_tensor(sm[:, 1, 5, :], sm[:, 1, 0, :], 1.0 / C, sm[:, 1, 1, :], ALU.mult, ALU.add).then_inc(s_w2, 1)
                if has(0):
                    newton(0, g, s_r1, s_n1)
                    wait(dve, s_xnt, g)
                    for b in range(NB):
                        last = v.tensor_scalar(xn_s[:, b, :], y_s[:, b, :], sm[:, 0, 3, b:b + 1], sm[:, 0, 10, b:b + 1],
                                               ALU.subtract, ALU.mult)
                    last.then_inc(s_xn, 1)
                if has(4):
                    q, sl = g - 4, SLOT2[prv(c, 4)]
                    newton(2, q, s_r3, s_n3)
                    wait(dve, s_res, q - 1)
                    wait(dve, s_tnt, q - 1)
                    for b in range(NB):
                        last = v.tensor_scalar(tn_s[:, sl, b, :], t_s[:, sl, b, :], sm[:, 2, 3, b:b + 1], sm[:, 2, 10, b:b + 1],
                                               ALU.subtract, ALU.mult)
                    last.then_inc(s_tn, 1)
                if has(3):
                    q, sl = g - 3, SLOT2[prv(c, 3)]
                    newton(1, q, s_r2, s_n2)
                    wait(dve, s_res, q - 1)
                    v.tensor_tensor(t_s[:, sl], p7[:, 0:NB * (C + 1)].rearrange("p (b c) -> p b c", b=NB)[:, :, 0:C],
                                    sm[:, 1, 10, :].unsqueeze(2).to_broadcast([128, NB, C]), ALU.mult).then_inc(s_t, 1)
                if has(6):
                    q, cq = g - 6, prv(c, 6)
                    wait(dve, s_l, q + 1)
                    v.tensor_copy(logits[:, cq * NB:(cq + 1) * NB, :], p01[:, 1, 0:NB * E].rearrange("p (b e) -> p b e", b=NB)).then_inc(s_ls, 1)
                    if cq == 6:
                        route(g, c)

            T = NB * CPI

            def route(g, c):
                im = (g - 12) // 7 if isinstance(g, int) else cur["i"]
                steps = 12
                k = [0]

                def then(ins):
                    k[0] += 1
                    ins.then_inc(s_top, 1)
                    wait(dve, s_top, im * steps + k[0])

                def over_e(x):
                    return x.unsqueeze(2).to_broadcast([128, T, E])

                ranks = rank[:, :].unsqueeze(1).to_broadcast([128, T, E])
                wait(dve, s_ls, (im + 1) * 7)
                for r in range(2):
                    val = logits[:, :, :] if r == 0 else pick[:, 2]
                    then(v.tensor_reduce(top[:, r, :], val, AX.X, ALU.max))
                    then(v.tensor_tensor(pick[:, r], val, over_e(top[:, r, :]), ALU.is_equal))
                    then(v.tensor_tensor(pick[:, r], pick[:, r], ranks, ALU.mult))
                    then(v.tensor_reduce(top[:, 4, :], pick[:, r], AX.X, ALU.max))
                    then(v.tensor_tensor(pick[:, r], pick[:, r], over_e(top[:, 4, :]), ALU.is_equal))
                    if r == 0:
                        then(v.scalar_tensor_tensor(pick[:, 2], pick[:, 0], -1e30, logits[:, :, :], ALU.mult, ALU.add))
                v.tensor_tensor(top[:, 2, :], top[:, 1, :], top[:, 0, :], ALU.subtract).then_inc(s_gap, 1)
                wait(dve, s_gexp, im + 1)
                then(v.tensor_scalar(top[:, 0, :], top[:, 3, :], 1.0, None, ALU.add))
                v.reciprocal(top[:, 1, :], top[:, 0, :]).then_inc(s_comb2, 1)
                wait(dve, s_comb2, im * 3 + 1)
                v.tensor_tensor(top[:, 2, :], top[:, 3, :], top[:, 1, :], ALU.mult)
                v.tensor_tensor(pick[:, 0], pick[:, 0], over_e(top[:, 1, :]), ALU.mult).then_inc(s_comb2, 1)
                wait(dve, s_comb2, im * 3 + 2)
                v.tensor_tensor(pick[:, 1], pick[:, 1], over_e(top[:, 2, :]), ALU.mult).then_inc(s_comb2, 1)
                wait(dve, s_comb2, im * 3 + 3)
                v.tensor_tensor(comb[:, bass.ds(im * (T * E), T * E)].rearrange("p (t e) -> p t e", e=E),
                                pick[:, 0], pick[:, 1], ALU.add).then_inc(s_comb, 1)

            cur = {}

            def walk_dve():
                for c in range(7):
                    step(c, c, lambda d, c=c: d <= c)
                with dve.Fori(1, G // 7) as i:
                    for c in range(7):
                        cur["i"] = i - 1 if c < 6 else i
                        step(i * 7 + c, c, lambda d: True)
                for c in range(7):
                    step(G + c, c, lambda d, c=c: d > c)

            walk_dve()

            def ct_copy(g, c):
                wait(dve, s_ct, g + 1)
                v.tensor_copy(ct_s[0:H * CP, c, :], p7[0:H * CP, 0:CH]).then_inc(s_cts, 1)

            def low(g, c):
                wait(dve, s_hi, g + 1)
                v.tensor_tensor(thl[64:128, c], tdup[64:128, c].rearrange("p (h n) -> p h n", h=H),
                                thl[64:128, c].bitcast(f32), ALU.subtract).then_inc(s_lo, 1)

            def parts_step(g, c, k):
                src = comb[:, bass.ds(g * (NB * E), NB * E)].rearrange("p (b e) -> p b e", b=NB)
                parts = cparts[:, c].rearrange("p (b k e) -> p k b e", b=NB, k=CP // E)
                if k == 0:
                    wait(dve, s_ct, g - 1)
                    v.tensor_scalar(parts[:, 0], src, 1.0, None, ALU.mult).then_inc(s_cs, 1)
                else:
                    wait(dve, s_cs, g * 4 + k)
                if k == 1:
                    v.tensor_tensor(cr, src, parts[:, 0], ALU.subtract).then_inc(s_cs, 1)
                if k == 2:
                    v.tensor_copy(parts[:, 1], cr).then_inc(s_cs, 1)
                if k == 3:
                    v.tensor_tensor(cf, cr, parts[:, 1], ALU.subtract).then_inc(s_cs, 1)
                if k == 4:
                    v.tensor_copy(parts[:, 2], cf).then_inc(s_cpt, 1)

            def step3(g, c, has, more=True):
                if has(0):
                    for j in range(4):
                        u = g * 4 + j
                        if more:
                            parts_step(g + 1, 1 - c, j)
                            if j == 3:
                                parts_step(g + 1, 1 - c, 4)
                                low(g + 1, 1 - c)
                        wait(dve, s_g, u + 1)
                        wait(dve, s_c, u + 1)
                        wait(dve, s_l2, u - 1)
                        v.tensor_tensor(gated[:, j % 2, :].rearrange("p (h n) -> p h n", h=H),
                                        hid[:, j % 2, :].rearrange("p (h n) -> p h n", h=H),
                                        p01[:, :, 0:CH], ALU.mult).then_inc(s_gm, 1)
                if has(1):
                    q, cq = g - 1, 1 - c
                    wait(dve, s_tt, q + 1)
                    stored(dve, q, cq)
                    v.tensor_tensor(fin[:, cq, :], p7[:, 0:CH], resid[:, bass.ds(q * CH, CH)], ALU.add).then_inc(s_fin, 1)
                if has(0) and more:
                    ct_copy(g + 1, 1 - c)

            def stored(eng, q, cq):
                if isinstance(q, int):
                    wait(eng, s_out[cq], 32 * (q // 2))
                else:
                    wait(eng, s_out[cq], 32 * cur["fin"])

            low(0, 0)
            dve.wait_ge(s_zero, 3)
            for k in range(5):
                parts_step(0, 0, k)
            ct_copy(0, 0)
            for g in range(4):
                step3(g, g % 2, lambda d, g=g: d <= g)
            with dve.Fori(2, G // 2 - 1) as i:
                cur["fin"] = i - 1
                step3(i * 2, 0, lambda d: True)
                cur["fin"] = i
                step3(i * 2 + 1, 1, lambda d: True)
            step3(G - 2, 0, lambda d: True)
            step3(G - 1, 1, lambda d: True, more=False)
            step3(G, 0, lambda d: d > 0, more=False)

        @blk.tensor
        def _(pe):
            t = nc.tensor
            for n in range(NP):
                pe.wait_ge(s_x1[n % 2], 16 * (n // 2 + 1))
                for k in range(PTOK):
                    hh = (n * PTOK + k) % 2
                    tile = x1[:, n % 2, k * C:(k + 1) * C]
                    last = t.matmul(p34[64 * hh:64 * hh + 64, 0, 0:C], tile, tile,
                                    start=(n * PTOK + k < 2), stop=(n * PTOK + k >= NP * PTOK - 2))
                last.then_inc(s_gram, 1)
            pe.wait_ge(s_const, 16 * 11)
            pe.wait_ge(s_zero, 1)
            pe.wait_ge(s_cd, 2)
            t.matmul(p2[:, 0:C], ones, colsum2[:, 0, :], start=True, stop=True)
            t.matmul(p2[:, C:C + 1], colsum2.rearrange("p a b -> p (a b)"), ones[:, 0:1], start=True, stop=True)
            t.matmul(p2[:, 2 * C:3 * C], fold, gram, start=True, stop=True).then_inc(s_cp, 1)
            pe.wait_ge(s_cd, 9)
            t.matmul(p7[0:64, 0:1], group, small1[0:64, 1:2], start=True, stop=True).then_inc(s_cp, 1)
            for it in range(ITERS - 1):
                pe.wait_ge(s_cd, 14 + 2 * it)
                t.matmul(p2[0:64, 0:2 * C], psig[0:64, 0, :], psig[0:64].rearrange("p a b -> p (a b)"),
                         start=True, stop=True).then_inc(s_cp, 1)
                pe.wait_ge(s_cd, 15 + 2 * it)
                t.matmul(p7[0:64, 0:C], pq[0:64, 0, :], pq[0:64, 1, :], start=True, stop=True).then_inc(s_cp, 1)
            pe.wait_ge(s_cd, 14 + 2 * (ITERS - 1) + 5)
            t.matmul(p2[:, 0:C], fold[0:64, :], rmat[0:64], start=True, stop=True).then_inc(s_cp, 1)
            pe.wait_ge(s_prep, 1)

            def flip(dst, src, weights, width=BLK):
                for b in range(NB):
                    for h in range(H):
                        last = t.matmul(dst[64 * h:64 * h + 64, b * width:(b + 1) * width], src(b), weights(h),
                                        start=True, stop=True)
                return last

            def one(h):
                return eye[:, 64 * h:64 * h + 64]

            def step(g, c, has):
                if has(0):
                    pe.wait_ge(s_x2[c], 32 * (g // 7 + 1) if isinstance(g, int) else 32 * (cur["i"] + 1))
                    wait(pe, s_tnts, g - 5)
                    flip(p01[:, 0], lambda b: x2[:, SLOT3[c], b * C:(b + 1) * C], one).then_inc(s_xt, 1)
                if has(1):
                    q = g - 1
                    wait(pe, s_xn, q + 1)
                    wait(pe, s_xnts, q)
                    flip(p2, lambda b: xn_s[:, b, :], one).then_inc(s_xnt, 1)
                if has(0):
                    wait(pe, s_xts, g + 1)
                    wait(pe, s_ls, g - 6)
                    flip(p01[:, 1], lambda b: xt_s[:, b * BLK:(b + 1) * BLK], lambda h: white[:, h, :]).then_inc(s_y, 1)
                if has(3):
                    q = g - 3
                    wait(pe, s_pm, q + 1)
                    wait(pe, s_vs, q + 1)
                    wait(pe, s_t, q)
                    for b in range(NB):
                        for h in range(H):
                            last = t.matmul(p7[64 * h:64 * h + 64, b * (C + 1):(b + 1) * (C + 1)],
                                            prob[:, h, b * BLK:(b + 1) * BLK], v_s[:, b, h, :], start=True, stop=True)
                    last.then_inc(s_o, 1)
                if has(2):
                    q, cq = g - 2, prv(c, 2)
                    wait(pe, s_xnts, q + 2 if has(1) else q + 1)
                    wait(pe, s_vs, q)
                    for b in range(NB):
                        last = t.transpose(p56[0:KEYS, b // 4, (b % 4) * 128:(b % 4 + 1) * 128],
                                           keys_t[:, cq, b * BLK:b * BLK + KEYS], eye[:, :])
                    last.then_inc(s_v, 1)
                    wait(pe, s_p, q)
                    for b in range(NB):
                        for lo, hi in ((0, BLK), (BLK, KEYS)):
                            for h in range(H):
                                last = t.matmul(p34[lo:hi, h, b * BLK:(b + 1) * BLK],
                                                keys_t[:, cq, b * BLK + lo:b * BLK + hi],
                                                qry[h][:, SLOT2[cq], b * BLK:(b + 1) * BLK], start=True, stop=True)
                    last.then_inc(s_s, 1)
                if has(5):
                    q, sl = g - 5, SLOT2[prv(c, 5)]
                    wait(pe, s_tn, q + 1)
                    if has(0):
                        wait(pe, s_xts, g + 1)
                    else:
                        wait(pe, s_tnts, q)
                    flip(p01[:, 0], lambda b: tn_s[:, sl, b, :], one).then_inc(s_tnt, 1)
                if has(6):
                    q, sl = g - 6, SLOT2[prv(c, 6)]
                    wait(pe, s_tnts, q + 1)
                    if has(0):
                        wait(pe, s_ys, g + 1)
                    else:
                        wait(pe, s_ls, q)
                    flip(p01[:, 1], lambda b: tnt_s[:, sl, b * BLK:(b + 1) * BLK], lambda h: router[:, h, :], E).then_inc(s_l, 1)

            cur = {}
            for c in range(7):
                step(c, c, lambda d, c=c: d <= c)
            with pe.Fori(1, G // 7) as i:
                cur["i"] = i
                for c in range(7):
                    step(i * 7 + c, c, lambda d: True)
            for c in range(7):
                step(G + c, c, lambda d, c=c: d > c)

            pe.wait_ge(s_p, G)
            pe.wait_ge(s_vs, G)
            pe.wait_ge(s_t, G)
            pe.wait_ge(s_ls, G)
            pe.wait_ge(s_xnts, G)

            def comb_t(g, c):
                wait(pe, s_cpt, g + 1)
                wait(pe, s_fin, g - 1)
                for b in range(NB):
                    for h in range(H):
                        last = t.matmul(p7[CP * h:CP * h + CP, b * BLK:(b + 1) * BLK],
                                        cparts[:, c, b * CP:(b + 1) * CP], eye_h[:, 64 * h:64 * h + 64],
                                        start=True, stop=True)
                last.then_inc(s_ct, 1)

            def first_layer(g, c, j):
                u = g * 4 + j
                bank = p34 if j % 2 == 0 else p56
                if j == 0:
                    wait(pe, s_lo, g + 1)
                wait(pe, s_g, u - 1)
                for k, w in enumerate((w1_hi, w1_lo)):
                    for h in range(H):
                        last = t.matmul(bank[:, h, 0:CH], w[:, 128 * j:128 * (j + 1)], thl[:, c, h, :],
                                        start=(k == 0), stop=(k == 1))
                last.then_inc(s_h, 1)

            def spread(g, c, j):
                u = g * 4 + j
                if j == 0:
                    wait(pe, s_cts, g + 1)
                wait(pe, s_gm, u)
                for h in range(H):
                    last = t.matmul(p01[:, h, 0:CH], selector[:, (4 * h + j) * 128:(4 * h + j + 1) * 128],
                                    ct_s[:, c, :], start=True, stop=True)
                last.then_inc(s_c, 1)

            def second_layer(g, c, j):
                u = g * 4 + j
                if j == 0:
                    wait(pe, s_y3s, g)
                    for p in range(PARTS):
                        for h in range(H):
                            t.matmul(p2[64 * h:64 * h + 64, 0:CH], b2_p[:, p, C * h:C * h + C], ct_s[:, c, :],
                                     start=(p == 0), stop=False)
                wait(pe, s_gm, u + 1)
                for h in range(H):
                    last = t.matmul(p2[64 * h:64 * h + 64, 0:CH], w2_s[:, j, :], gated[:, j % 2, h * CH:(h + 1) * CH],
                                    start=False, stop=(j == 3))
                last.then_inc(s_l2, 1)

            def back(g, c):
                wait(pe, s_y3s, g + 1)
                wait(pe, s_cts, cur["cts"])
                wait(pe, s_fin, g)
                flip(p7, lambda b: y3[:, b * BLK:(b + 1) * BLK], one).then_inc(s_tt, 1)

            def step3(g, c, has, more=True):
                for j in range(4):
                    if has(0):
                        first_layer(g, c, j)
                    if j < 2:
                        if has(1):
                            second_layer(g - 1, 1 - c, j + 2)
                    elif has(0):
                        second_layer(g, c, j - 2)
                    if has(0):
                        spread(g, c, j)
                if has(1):
                    cur["cts"] = g + 1 if has(0) else G
                    back(g - 1, 1 - c)
                if has(0) and more:
                    comb_t(g + 1, 1 - c)

            comb_t(0, 0)
            step3(0, 0, lambda d: d <= 0)
            step3(1, 1, lambda d: d <= 1)
            with pe.Fori(1, G // 2 - 1) as i:
                step3(i * 2, 0, lambda d: True)
                step3(i * 2 + 1, 1, lambda d: True)
            step3(G - 2, 0, lambda d: True)
            step3(G - 1, 1, lambda d: True, more=False)
            step3(G, 0, lambda d: d > 0, more=False)


_INS = ['x', 'L0_conv_gamma', 'L0_conv_beta', 'L1_attn_gamma', 'L1_attn_beta', 'L1_ffn_router_w', 'L1_ffn_w1',
        'L1_ffn_b1', 'L1_ffn_w2', 'L1_ffn_b2']


def _constants(n_tokens):
    import numpy as np
    f = np.float32
    eye64 = np.eye(C, dtype=f)
    grp = np.kron(np.eye(C // M_GROUP, dtype=f), np.ones((M_GROUP, M_GROUP), f))
    block = np.tile(grp * f((1.0 - EPS_W) / (n_tokens - 1.0)), (2, 1))
    k, q = np.arange(KEYS)[:, None], np.arange(BLK)[None, :]
    band = ((k - q >= 0) & (k - q <= 2 * WIN)).astype(f)
    sel = np.zeros((128, H, 4, 2, C), f)
    for h in range(H):
        for p in range(PARTS):
            for e in range(E):
                sel[CP * h + E * p + e, h, e // 2, e % 2, :] = 1.0
    return {"eye": np.eye(128, dtype=f), "fold": np.tile(eye64, (2, 2)), "group": grp, "block": block,
            "band": band, "rank": np.arange(E, 0, -1).astype(f), "sel": sel.reshape(128, -1)}


def kernel(**inputs):
    import numpy as _np
    import concourse.bacc as _bacc
    from concourse import mybir as _mybir
    from concourse.bass_utils import run_bass_kernel_spmd as _run

    nc = _bacc.Bacc("TRN2", target_bir_lowering=False, num_devices=1)
    arrays, args = {}, []
    shape = inputs['x'].shape
    named = {n: inputs[n] for n in _INS}
    named.update({f"k_{n}": a for n, a in _constants(shape[0] * shape[1] * shape[2]).items()})
    for name, a in named.items():
        a = _np.ascontiguousarray(a)
        arrays[f"in_{name}_dram"] = a
        args.append(nc.dram_tensor(f"in_{name}_dram", a.shape, _mybir.dt.from_np(a.dtype), kind="ExternalInput").ap())
    args.append(nc.dram_tensor("out_0_dram", shape, _mybir.dt.float32, kind="ExternalOutput").ap())
    hybrid_kernel(nc, *args)
    r = _run(nc, [arrays], core_ids=[0])
    return r.results[0]["out_0_dram"]
```

```python
import concourse.bass as bass
from concourse import mybir
from contextlib import ExitStack

H = 2
BLK = 64
NB = 7
CH = NB * BLK
C = 64
WIN = 16
KEYS = BLK + 2 * WIN
E = 8
PARTS = 3
CP = 32
M_GROUP = 16
ITERS = 5
EPS_W = 1e-5
EPS_LN = 1e-5
SLOT2 = [0, 1, 0, 1, 0, 1, 2]
SLOT3 = [0, 1, 2, 0, 1, 2, 3]
ROUTE_GEXP = 3


def hybrid_kernel(nc, x, g0, b0, g1, b1v, rw, w1, b1, w2, b2, k_eye, k_fold, k_group, k_block, k_band,
                  k_rank, k_sel, out):
    f32, bf16, f32r = mybir.dt.float32, mybir.dt.bfloat16, mybir.dt.float32r
    ALU, ACT, AX = mybir.AluOpType, mybir.ActivationFunctionType, mybir.AxisListType
    IMGS, HH, WW, _ = x.shape
    NP = IMGS // H
    TOK = HH * WW
    CPI = TOK // CH
    G = NP * CPI
    N = IMGS * TOK
    PTOK = H * TOK // 128
    assert CPI == 7 and G % 2 == 0 and PTOK * 128 == H * TOK
    SCALE = float(C) ** -0.5

    x_flat = x.rearrange("i a b c -> (i a b c)")
    x_pairs = x_flat.rearrange("(n p f) -> n p f", n=NP, p=128)
    x_chunks = x_flat.rearrange("(h g b p c) -> h g p b c", h=H, g=G, b=NB, p=BLK)
    out_chunks = out.rearrange("i a b c -> (i a b c)").rearrange("(h g b p c) -> h g p b c", h=H, g=G, b=NB, p=BLK)
    spill = nc.dram_tensor("tn_spill", (G, 128, CH), f32).ap()

    ctx = ExitStack()
    with ctx:
        def sb(name, shape, dt=f32):
            return ctx.enter_context(nc.sbuf_tensor(name, shape, dt))

        def pb(name, shape):
            return ctx.enter_context(nc.psum_tensor(name, shape, f32))

        def sem(name):
            return ctx.enter_context(nc.semaphore(name))

        resid = sb("resid", [128, G * CH])
        comb = sb("comb", [128, G * NB * E])
        eye = sb("eye", [128, 128])
        band = sb("band", [KEYS, BLK])
        rank = sb("rank", [128, E])
        selector = sb("selector", [128, H * 4 * 128], bf16)
        eye_h = sb("eye_h", [128, 128], bf16)
        gam1 = sb("gam1", [128, C])
        bet1 = sb("bet1", [128, C])
        white = sb("white", [128, H, C])
        router = sb("router", [128, H, E])
        neg_mean = sb("neg_mean", [128, 1])
        w1_hi = sb("w1_hi", [128, E * C], f32r)
        w1_lo = sb("w1_lo", [128, E * C], f32r)
        w2_s = sb("w2_s", [128, 4, C])
        b1_s = sb("b1_s", [128, 4])
        b2_p = sb("b2_p", [128, PARTS, (H + 1) * C], bf16)
        bet0_rows = sb("bet0_rows", [128, H * C], bf16)
        ones_h = sb("ones_h", [128, 128], bf16)
        ARENA = 9840
        arena = sb("arena", [128, ARENA])
        logits = sb("logits", [128, NB * CPI, E])

        def carve(at, shape, dt=f32, rows=128):
            n = 1
            for s in shape:
                n *= s
            assert at[0] + (n if dt != bf16 else n // 2) <= ARENA, (at, n)
            view = arena[0:rows, at[0]:at[0] + (n if dt != bf16 else (n + 1) // 2)]
            at[0] += n if dt != bf16 else (n + 1) // 2
            if dt != f32:
                view = view.bitcast(dt)
            if len(shape) == 2:
                view = view.rearrange("p (a b) -> p a b", a=shape[0])
            if len(shape) == 3:
                view = view.rearrange("p (a b c) -> p a b c", a=shape[0], b=shape[1])
            return view

        at = [0]
        x1 = carve(at, [2, PTOK * C])
        colsum = carve(at, [NP, C])
        colsum2 = carve(at, [2, C])
        gram = carve(at, [C])
        srow = carve(at, [C])
        scol = carve(at, [1])
        outer = carve(at, [C])
        psig = carve(at, [2, C])
        pq = carve(at, [2, C])
        p15 = carve(at, [C])
        covd = carve(at, [C])
        small1 = carve(at, [16])
        rmat = carve(at, [C])
        sel_f = carve(at, [H * 4 * 128])
        w1_f = carve(at, [E * C])
        b2_f = carve(at, [(H + 1) * C])
        fold = carve(at, [128])
        ones = carve(at, [128])
        group = carve(at, [64], rows=64)
        block = carve(at, [64])
        gam0 = carve(at, [C], rows=64)
        at = [0]
        x2 = carve(at, [4, CH])
        keys_t = carve(at, [7, CH + 2 * WIN])
        qry = carve(at, [3, NB, H * BLK])
        at = [ARENA - 3 * NB * CPI * E]
        pick = carve(at, [3, NB * CPI * E]).rearrange("p k (t e) -> p k t e", e=E)
        at3 = [0]
        tdup = carve(at3, [2, H * CH])
        hid = carve(at3, [2, H * CH])
        gated = carve(at3, [2, H * CH])
        y3 = carve(at3, [CH])
        fin = carve(at3, [2, CH])
        ct_s = carve(at3, [2, CH], bf16)
        cf = carve(at3, [NB, E])
        cr = carve(at3, [NB, E])
        cparts = carve(at3, [2, NB * CP], bf16)

        with nc.sbuf_tensor("yb", [128, 7, CH], f32) as yb:
            pass
        thl = sb("thl", [128, 2, H, CH], f32r)
        sb("rest_of_yb", [128, 7 * CH - 2 * H * CH])
        xt_s = sb("xt_s", [128, CH])
        xn_s = sb("xn_s", [128, NB, C])
        v_s = sb("v_s", [KEYS, NB, H, C + 1])
        prob = sb("prob", [KEYS, NB, H * BLK])
        sq = sb("sq", [128, NB, C + 1])
        t_s = sb("t_s", [128, 3, NB, C])
        tn_s = sb("tn_s", [128, 3, NB, C])
        tnt_s = sb("tnt_s", [128, 3, CH])
        st = sb("st", [128, 2, NB, 6])
        sm = sb("sm", [128, 10, 3, NB])
        top = sb("top", [128, 5, NB * CPI])

        p01 = pb("p01", [128, 2, 512])
        p2 = pb("p2", [128, 512])
        p34 = pb("p34", [128, 2, 512])
        p56 = pb("p56", [128, 2, 512])
        p7 = pb("p7", [128, 512])

        s_const, s_weights, s_x1 = sem("consts_in"), sem("weights_in"), [sem(f"x1_in{i}") for i in range(2)]
        s_zero, s_prep, s_prep_pool = sem("zeroed"), sem("prep_done"), sem("prep_pool")
        s_gram, s_colsum = sem("gram_done"), sem("colsum_done")
        s_cd, s_cp, s_ca = sem("chain_dve"), sem("chain_pe"), sem("chain_act")
        s_x2 = [sem(f"x2_in{i}") for i in range(7)]
        s_xt, s_xts, s_y, s_ys, s_yb = sem("xt"), sem("xt_copied"), sem("y"), sem("y_copied"), sem("yb")
        s_v, s_w, s_ln, s_r, s_n = sem("norm_steps"), sem("norm_var"), sem("norm_log"), sem("norm_rsqrt"), sem("norm_newton")
        s_xc, s_xn = sem("y_centred"), sem("xn")
        s_xnt, s_kts, s_xnts = sem("xn_t"), sem("keys_copied"), sem("keys_and_queries_copied")
        s_vt, s_vs, s_s, s_p, s_pm, s_o = sem("v"), sem("v_copied"), sem("scores"), sem("probs"), sem("probs_masked"), sem("pv")
        s_sq, s_t = sem("pv_squared"), sem("t_scaled")
        s_tp, s_t2 = sem("t_gamma"), sem("t2")
        s_tc, s_tn = sem("t_centred"), sem("tn")
        s_res, s_tnt, s_tnts, s_l, s_ls = sem("resid"), sem("tn_t"), sem("tn_t_copied"), sem("logits"), sem("logits_copied")
        s_sp = [sem(f"spilled{i}") for i in range(3)]
        s_top, s_gap, s_gexp, s_comb = sem("top_steps"), sem("top_gap"), sem("top_exp"), sem("combined")
        s_td = [sem(f"tdup_in{i}") for i in range(2)]
        s_hi, s_lo, s_cs, s_cpt = sem("tn_hi"), sem("tn_lo"), sem("comb_steps"), sem("comb_parts")
        s_ct, s_cts = sem("comb_t"), sem("comb_t_copied")
        s_h, s_g, s_c, s_gm = sem("hidden"), sem("gelu"), sem("weights_spread"), sem("gated")
        s_l2, s_y3s, s_tt, s_fin = sem("second_layer"), sem("expert_sum_copied"), sem("back_t"), sem("fin")
        s_out = [sem(f"stored{i}") for i in range(2)]

        def wait(eng, s, n):
            if not isinstance(n, int) or n > 0:
                eng.wait_ge(s, n)

        def walk(eng, step, period, chunks, skew):
            assert chunks % period == 0 and skew <= period
            for c in range(period):
                step(c, c, lambda d, c=c: d <= c)
            with eng.Fori(1, chunks // period) as i:
                for c in range(period):
                    step(i * period + c, c, lambda d: True)
            for c in range(skew):
                step(chunks + c, c, lambda d, c=c: d > c)

        def prv(c, d, n=7):
            return (c - d) % n

        def norms(has):
            lo = 0 if has(0) else 1 if has(3) else 2
            hi = 3 if has(4) else 2 if has(3) else 1
            return lo, hi

        def route_image(g, c):
            im = g // 7 - (1 if c == 6 else 2)
            return im if 0 <= im < NP and c != 5 else None

        blk = ctx.enter_context(nc.Block())

        @blk.sync
        def _(sp):
            sp.dma_start(x1[:, 0, :], x_pairs[0]).then_inc(s_x1[0], 16)
            sp.dma_start(x1[:, 1, :], x_pairs[1]).then_inc(s_x1[1], 16)
            for dst, src in ((eye[:, :], k_eye), (fold, k_fold), (group, k_group),
                             (block, k_block), (band[:, :], k_band),
                             (rank[:, :], k_rank.partition_broadcast(128)), (sel_f[:, :], k_sel),
                             (gam0, g0.rearrange("a b c d -> (a b c d)").partition_broadcast(64)),
                             (b2_f[:, H * C:], b0.rearrange("a b c d -> (a b c d)").partition_broadcast(128)),
                             (gam1[:, :], g1.partition_broadcast(128)),
                             (bet1[:, :], b1v.partition_broadcast(128))):
                sp.dma_start(dst, src).then_inc(s_const, 16)
            with sp.Fori(1, NP // 2) as i:
                for k in range(2):
                    n = i * 2
                    sp.wait_ge(s_gram, n + k - 1)
                    sp.wait_ge(s_colsum, n + k - 1)
                    sp.dma_start(x1[:, k, :], x_pairs[n + k]).then_inc(s_x1[k], 16)
            sp.wait_ge(s_gram, NP)
            sp.wait_ge(s_colsum, NP)

            def step(g, c, has):
                if has(0):
                    wait(sp, s_xt, g - 2)
                    for h in range(H):
                        sp.dma_start(x2[64 * h:64 * h + 64, SLOT3[c], :].rearrange("p (b c) -> p b c", b=NB),
                                     x_chunks[h, g]).then_inc(s_x2[c], 16)

            walk(sp, step, 7, G, 0)

            sp.wait_ge(s_xt, G)

            def step3(g, c, has):
                if has(0):
                    wait(sp, s_hi, g - 1)
                    wait(sp, s_lo, g - 1)
                    for d in range(2):
                        sp.dma_start(tdup[64 * d:64 * d + 64, c, :].rearrange("p (h n) -> p h n", h=H),
                                     spill[g].rearrange("(h p) n -> p h n", h=H)).then_inc(s_td[c], 16)
                if has(2):
                    wait(sp, s_fin, g - 1)
                    for h in range(H):
                        sp.dma_start(out_chunks[h, g - 2], fin[64 * h:64 * h + 64, c, :].rearrange("p (b c) -> p b c", b=NB))\
                          .then_inc(s_out[c], 16)

            for c in range(2):
                sp.wait_ge(s_sp[c], 16)
                step3(c, c, lambda d: d == 0)
            for k in range(3):
                spilled = sum(1 for c in range(7) if SLOT2[c] == k) * NP
                sp.wait_ge(s_sp[k], 16 * spilled)
            sp.wait_ge(s_s, G)
            with sp.Fori(1, G // 2) as i:
                for c in range(2):
                    step3(i * 2 + c, c, lambda d: True)
            for c in range(2):
                step3(G + c, c, lambda d: d > 0)
            for c in range(2):
                sp.wait_ge(s_out[c], 32 * (G // 2))

        @blk.gpsimd
        def _(pool):
            v = nc.gpsimd
            for dst, src in ((w1_f[0:64, :].rearrange("d (e f) -> d e f", e=E), w1.rearrange("e d f -> d e f")),
                             (w1_f[64:128, :].rearrange("d (e f) -> d e f", e=E), w1.rearrange("e d f -> d e f")),
                             (w2_s[:, :, :], w2.rearrange("(j e) f d -> (e f) j d", e=2)),
                             (b1_s[:, :], b1.rearrange("(j e) f -> (e f) j", e=2))):
                pool.dma_start(dst, src, allow_slow_non_contiguous=True).then_inc(s_weights, 16)
            v.memset(router[:, :, :], 0.0)
            v.memset(b2_f[:, 0:H * C], 0.0)
            v.memset(bet0_rows[:, :], 0.0)
            v.memset(ones_h[:, :], 1.0)
            v.memset(white[:, :, :], 0.0)
            v.memset(ones, 1.0)
            v.memset(v_s[:, :, :, :], 1.0).then_inc(s_zero, 1)
            pool.wait_ge(s_zero, 1)
            for h in range(H):
                pool.dma_start(router[64 * h:64 * h + 64, h, :], rw.rearrange("e c -> c e"),
                               allow_slow_non_contiguous=True).then_inc(s_weights, 16)
                for p in range(PARTS):
                    r = CP * h + E * p
                    pool.dma_start(b2_f[r:r + E, C * h:C * h + C], b2).then_inc(s_weights, 16)
            pool.wait_ge(s_weights, 16 * (4 + H * (1 + PARTS)))
            pool.wait_ge(s_const, 16 * 11)
            n = 0
            v.tensor_copy(selector[:, :], sel_f)
            v.tensor_copy(eye_h[:, :], eye[:, :])
            for p in range(PARTS):
                v.tensor_copy(b2_p[:, p, :], b2_f).then_inc(s_prep_pool, 1)
                n += 1
                pool.wait_ge(s_prep_pool, n)
                if p < PARTS - 1:
                    v.tensor_tensor(b2_f, b2_f, b2_p[:, p, :], ALU.subtract).then_inc(s_prep_pool, 1)
                    n += 1
                    pool.wait_ge(s_prep_pool, n)
            for p in range(PARTS):
                r = slice(32 * p, 32 * p + 1)
                v.tensor_copy(bet0_rows[r, :].rearrange("p (b c) -> p b c", b=2),
                              b2_p[r, p, H * C:].unsqueeze(1).to_broadcast([1, 2, C])).then_inc(s_prep_pool, 1)
                n += 1
                pool.wait_ge(s_prep_pool, n)

            pool.wait_ge(s_prep, 1)
            v.memset(qry, 0.0)
            v.memset(keys_t[:, 0, 0:WIN], 0.0)
            v.memset(keys_t[:, 6, WIN + CH:], 0.0).then_inc(s_zero, 1)

            def step(g, c, has):
                if has(5):
                    q, sl = g - 5, SLOT2[prv(c, 5)]
                    wait(pool, s_tn, q + 1)
                    v.tensor_tensor(resid[:, bass.ds(q * CH, CH)], t_s[:, sl].rearrange("p b c -> p (b c)"),
                                    tn_s[:, sl].rearrange("p b c -> p (b c)"), ALU.add).then_inc(s_res, 1)
                if has(2):
                    q = g - 2
                    wait(pool, s_p, q + 1)
                    pv = prob[:, :, :].rearrange("p b (h q) -> p (b h) q", h=H)
                    v.tensor_tensor(pv, pv, band[:, :].unsqueeze(1).to_broadcast([KEYS, H * NB, BLK]),
                                    ALU.mult).then_inc(s_pm, 1)
                if has(3):
                    q, cq = g - 3, prv(c, 3)
                    sl = SLOT2[cq]
                    wait(pool, s_t, q + 1)
                    v.tensor_tensor(t_s[:, sl], t_s[:, sl], gam1[:, :].unsqueeze(1).to_broadcast([128, NB, C]),
                                    ALU.mult).then_inc(s_tp, 1)
                    wait(pool, s_tp, q + 1)
                    wait(pool, s_yb, q + 1)
                    v.tensor_tensor(t_s[:, sl], t_s[:, sl], yb[:, cq].rearrange("p (b c) -> p b c", b=NB),
                                    ALU.add).then_inc(s_t2, 1)
                if has(0):
                    wait(pool, s_xc, g + 1)
                    ybc = yb[:, c].rearrange("p (b c) -> p b c", b=NB)
                    v.tensor_tensor(ybc, ybc, bet1[:, :].unsqueeze(1).to_broadcast([128, NB, C]), ALU.add).then_inc(s_yb, 1)

            walk(pool, step, 7, G, 5)

            pool.wait_ge(s_s, G)
            v.memset(ct_s, 0.0)
            v.memset(cparts, 0.0).then_inc(s_zero, 1)

        @blk.scalar
        def _(act):
            a = nc.scalar
            a.preload_act_table_set("natural_log_exp_and_others")
            act.wait_ge(s_weights, 16 * (4 + H * (1 + PARTS)))
            a.activation(w1_hi[:, :], w1_f, ACT.Copy).then_inc(s_ca, 1)
            act.wait_ge(s_cd, 10)
            a.activation(small1[0:64, 3:4], small1[0:64, 0:1], ACT.Ln).then_inc(s_ca, 1)
            act.wait_ge(s_ca, 2)
            a.activation(small1[0:64, 4:5], small1[0:64, 3:4], ACT.Exp, scale=-0.5).then_inc(s_ca, 1)

            act.wait_ge(s_prep, 1)

            def step(g, c, has):
                if has(0):
                    wait(act, s_xt, g + 1)
                    wait(act, s_y, g)
                    a.activation(xt_s[:, :], p01[:, 0, 0:CH], ACT.Identity, bias=neg_mean[:, :]).then_inc(s_xts, 1)
                if has(6):
                    q, cq = g - 6, prv(c, 6)
                    wait(act, s_l, q + 1)
                    if cq == 0:
                        before = q // 7 - 1 if isinstance(q, int) else cur["period"] - 1
                        if not isinstance(before, int) or before >= 0:
                            wait(act, s_top, before * 17 + 1)
                    a.activation(logits[:, cq * NB:(cq + 1) * NB, :], p2[:, CH:CH + NB * E].rearrange("p (b e) -> p b e", b=NB),
                                 ACT.Copy).then_inc(s_ls, 1)
                if has(0):
                    wait(act, s_y, g + 1)
                    wait(act, s_t2, g - 6)
                    a.activation(yb[:, c, :], p01[:, 1, 0:CH], ACT.Copy).then_inc(s_ys, 1)
                if has(1):
                    q, cq = g - 1, prv(c, 1)
                    wait(act, s_xnt, q + 1)
                    wait(act, s_s, q - 1)
                    if isinstance(q, int) and q == 0:
                        act.wait_ge(s_zero, 2)
                    if cq < 6:
                        a.activation(keys_t[:, cq + 1, 0:WIN], p2[:, CH - WIN:CH], ACT.Copy)
                    if cq > 0:
                        a.activation(keys_t[:, cq - 1, WIN + CH:], p2[:, 0:WIN], ACT.Copy)
                    a.activation(keys_t[:, cq, WIN:WIN + CH], p2[:, 0:CH], ACT.Copy).then_inc(s_kts, 1)
                    for h in range(H):
                        r = slice(64 * h, 64 * h + 64)
                        last = a.activation(qry[r, SLOT2[cq], :, 64 * h:64 * h + 64], p2[r, 0:CH].rearrange("p (b q) -> p b q", b=NB), ACT.Copy)
                    last.then_inc(s_xnts, 1)
                if has(3):
                    q = g - 3
                    wait(act, s_o, q + 1)
                    wait(act, s_w, g)
                    a.activation(sq[:, :, :], p7[:, 0:NB * (C + 1)].rearrange("p (b c) -> p b c", b=NB),
                                 ACT.Square).then_inc(s_sq, 1)
                if has(2):
                    q = g - 2
                    wait(act, s_vt, q + 1)
                    wait(act, s_o, q)
                    for k, (lo, n) in enumerate(((0, 4), (4, 3))):
                        last = a.activation(v_s[:, lo:lo + n, :, 0:C],
                                            p56[0:KEYS, k, 0:n * 128].rearrange("p (b h c) -> p b h c", b=n, h=H),
                                            ACT.Copy)
                    last.then_inc(s_vs, 1)
                if has(5):
                    q, sl = g - 5, SLOT2[prv(c, 5)]
                    wait(act, s_tnt, q + 1)
                    wait(act, s_l, q - 1)
                    if not isinstance(q, int) or q >= 2:
                        uses = sum(1 for k in range(prv(c, 5)) if SLOT2[k] == sl)
                        per = sum(1 for k in range(7) if SLOT2[k] == sl)
                        n = (q - prv(c, 5)) // 7 * per + uses if isinstance(q, int) else None
                        if n is None:
                            n = spill_count(q, prv(c, 5), per, uses)
                        wait(act, s_sp[sl], 16 * n)
                    a.activation(tnt_s[:, sl, :], p01[:, 0, 0:CH], ACT.Copy).then_inc(s_tnts, 1)
                    wait(act, s_tnts, q + 1)
                    act.dma_start(spill[q], tnt_s[:, sl, :]).then_inc(s_sp[sl], 16)
                im = image_routed(g, c)
                if c == ROUTE_GEXP and im is not None:
                    wait(act, s_gap, im + 1)
                    a.activation(top[:, 3, :], top[:, 2, :], ACT.Exp).then_inc(s_gexp, 1)
                lo, hi = norms(has)
                if lo < hi:
                    wait(act, s_w, g + 1)
                    a.activation(sm[:, 6, lo:hi, :], sm[:, 5, lo:hi, :], ACT.Ln).then_inc(s_ln, 1)
                    wait(act, s_ln, g + 1)
                    a.activation(sm[:, 7, lo:hi, :], sm[:, 6, lo:hi, :], ACT.Exp, scale=-0.5).then_inc(s_r, 1)
                if has(2):
                    q = g - 2
                    wait(act, s_s, q + 1)
                    a.activation(prob[:, :, :].rearrange("p b q -> p (b q)"),
                                 p34[0:KEYS].rearrange("p a n -> p (a n)")[:, 0:NB * H * BLK], ACT.Exp, scale=SCALE).then_inc(s_p, 1)

            cur = {}

            def spill_count(q, cq, per, uses):
                return cur["i"](cq) * per + uses

            def image_routed(g, c):
                return route_image(g, c) if isinstance(g, int) else cur["period"] - (1 if c == 6 else 2)

            def walk_act():
                for g in range(14):
                    step(g, g % 7, lambda d, g=g: d <= g)
                with act.Fori(2, G // 7) as i:
                    for c in range(7):
                        cur["i"] = lambda cq, c=c: i if cq <= c else i - 1
                        cur["period"] = i
                        step(i * 7 + c, c, lambda d: True)
                for c in range(7):
                    step(G + c, c, lambda d, c=c: d > c)

            walk_act()

            def gelu(g, c, j):
                u = g * 4 + j
                wait(act, s_h, u + 1)
                wait(act, s_gm, u - 1)
                a.activation(hid[:, j % 2, :].rearrange("p (h n) -> p h n", h=H),
                             (p34 if j % 2 == 0 else p56)[:, :, 0:CH], ACT.Gelu, bias=b1_s[:, j:j + 1]).then_inc(s_g, 1)

            def high(g, c):
                if isinstance(g, int) and g >= G:
                    return
                n = cur["round"](g)
                wait(act, s_td[c], 32 * n)
                wait(act, s_h, 4 * (g - 1))
                a.activation(thl[:, c], tdup[:, c].rearrange("p (h n) -> p h n", h=H), ACT.Copy).then_inc(s_hi, 1)

            def step3(g, c, has, i):
                if has(0):
                    gelu(g, c, 0)
                    gelu(g, c, 1)
                if has(1):
                    wait(act, s_l2, 4 * g)
                    wait(act, s_tt, g - 1)
                    a.activation(y3, p2[:, 0:CH], ACT.Copy).then_inc(s_y3s, 1)
                if has(0):
                    gelu(g, c, 2)
                    if not (isinstance(g, int) and g + 1 >= G):
                        cur["round"] = lambda _: (i + 1 if c == 0 else i + 2)
                        high(g + 1, 1 - c)
                    gelu(g, c, 3)

            cur["round"] = lambda _: 1
            high(0, 0)
            step3(0, 0, lambda d: d <= 0, 0)
            act.wait_ge(s_gap, NP)
            a.activation(top[:, 3, :], top[:, 2, :], ACT.Exp).then_inc(s_gexp, 1)
            step3(1, 1, lambda d: d <= 1, 0)
            with act.Fori(1, G // 2 - 1) as i:
                step3(i * 2, 0, lambda d: True, i)
                step3(i * 2 + 1, 1, lambda d: True, i)
            step3(G - 2, 0, lambda d: True, G // 2 - 1)
            step3(G - 1, 1, lambda d: True, G // 2 - 1)
            step3(G, 0, lambda d: d > 0, G // 2)

        @blk.vector
        def _(dve):
            v = nc.vector
            n_cd = [0]

            def link(ins):
                n_cd[0] += 1
                ins.then_inc(s_cd, 1)
                dve.wait_ge(s_cd, n_cd[0])

            for k in range(2):
                dve.wait_ge(s_x1[k], 16)
                v.tensor_reduce(colsum[:, k, :], x1[:, k, :].rearrange("p (t c) -> p c t", c=C), AX.X, ALU.add).then_inc(s_colsum, 1)
            for n in range(2, NP):
                dve.wait_ge(s_x1[n % 2], 16 * (n // 2 + 1))
                v.tensor_reduce(colsum[:, n, :], x1[:, n % 2, :].rearrange("p (t c) -> p c t", c=C), AX.X, ALU.add).then_inc(s_colsum, 1)
            dve.wait_ge(s_colsum, NP)
            for k in range(2):
                last = v.tensor_reduce(colsum2[:, k, :], colsum.rearrange("p n c -> p c n"), AX.X, ALU.add)
            link(last)
            dve.wait_ge(s_gram, NP)
            link(v.tensor_copy(gram, p34[:, 0, 0:C]))
            dve.wait_ge(s_cp, 1)
            v.tensor_copy(scol, p2[:, C:C + 1])
            link(v.tensor_copy(srow, p2[:, 0:C]))
            v.tensor_scalar(neg_mean[:, :], scol, -1.0 / N, None, ALU.mult)
            link(v.tensor_scalar(outer, srow, scol, -1.0 / N, ALU.mult, ALU.mult))
            link(v.tensor_tensor(outer, outer, p2[:, 2 * C:3 * C], ALU.add))
            link(v.tensor_tensor(outer, outer, block, ALU.mult))
            link(v.scalar_tensor_tensor(covd[0:64], eye[0:64, 0:64], EPS_W, outer[0:64], ALU.mult, ALU.add))
            link(v.tensor_tensor(p15[0:64], covd[0:64], eye[0:64, 0:64], ALU.mult))
            link(v.tensor_reduce(small1[0:64, 1:2], p15[0:64], AX.X, ALU.add))
            dve.wait_ge(s_cp, 2)
            link(v.tensor_copy(small1[0:64, 0:1], p7[0:64, 0:1]))
            link(v.reciprocal(small1[0:64, 2:3], small1[0:64, 0:1]))
            link(v.tensor_scalar(psig[0:64, 1, :], covd[0:64], small1[0:64, 2:3], None, ALU.mult))
            link(v.tensor_scalar(p15[0:64], eye[0:64, 0:64], 1.5, None, ALU.mult))
            link(v.scalar_tensor_tensor(psig[0:64, 0, :], psig[0:64, 1, :], -0.5, p15[0:64], ALU.mult, ALU.add))
            for it in range(ITERS - 1):
                dve.wait_ge(s_cp, 3 + 2 * it)
                v.tensor_scalar(p15[0:64], psig[0:64, 0, :], 1.5, None, ALU.mult)
                link(v.tensor_copy(pq[0:64].rearrange("p a b -> p (a b)"), p2[0:64, 0:2 * C]))
                dve.wait_ge(s_cp, 4 + 2 * it)
                link(v.scalar_tensor_tensor(psig[0:64, 0, :], p7[0:64, 0:C], -0.5, p15[0:64], ALU.mult, ALU.add))
            dve.wait_ge(s_ca, 3)
            link(v.tensor_tensor(small1[0:64, 5:6], small1[0:64, 0:1], small1[0:64, 4:5], ALU.mult))
            link(v.scalar_tensor_tensor(small1[0:64, 6:7], small1[0:64, 5:6], -0.5, small1[0:64, 4:5], ALU.mult, ALU.mult))
            link(v.scalar_tensor_tensor(small1[0:64, 7:8], small1[0:64, 6:7], 1.5, small1[0:64, 4:5], ALU.add, ALU.mult))
            link(v.tensor_scalar(rmat[0:64], psig[0:64, 0, :], small1[0:64, 7:8], None, ALU.mult))
            link(v.tensor_tensor(rmat[0:64], rmat[0:64], gam0, ALU.mult))
            v.tensor_tensor(w1_lo[:, :], w1_f, w1_hi[:, :].bitcast(f32), ALU.subtract)
            dve.wait_ge(s_cp, 3 + 2 * (ITERS - 1))
            dve.wait_ge(s_zero, 1)
            v.tensor_copy(white[0:64, 0, :], p2[0:64, 0:C])
            dve.wait_ge(s_prep_pool, 3 * PARTS - 1)
            v.tensor_copy(white[64:128, 1, :], p2[64:128, 0:C]).then_inc(s_prep, 1)

            T = NB * CPI

            def route(im, k):
                if k == 12:
                    wait(dve, s_gexp, im + 1)
                else:
                    wait(dve, s_top, im * 17 + (k + 1 if k < 12 else k))
                val = pick[:, 2]
                r = 0 if k < 6 else 1

                def over_e(x):
                    return x.unsqueeze(2).to_broadcast([128, T, E])

                if k in (0, 6):
                    ins = v.tensor_reduce(top[:, r, :], val, AX.X, ALU.max)
                if k in (1, 7):
                    ins = v.tensor_tensor(pick[:, r], val, over_e(top[:, r, :]), ALU.is_equal)
                if k in (2, 8):
                    ins = v.tensor_tensor(pick[:, r], pick[:, r], rank[:, :].unsqueeze(1).to_broadcast([128, T, E]), ALU.mult)
                if k in (3, 9):
                    ins = v.tensor_reduce(top[:, 4, :], pick[:, r], AX.X, ALU.max)
                if k in (4, 10):
                    ins = v.tensor_tensor(pick[:, r], pick[:, r], over_e(top[:, 4, :]), ALU.is_equal)
                if k == 5:
                    ins = v.scalar_tensor_tensor(val, pick[:, 0], -1e30, val, ALU.mult, ALU.add)
                if k == 11:
                    v.tensor_tensor(top[:, 2, :], top[:, 1, :], top[:, 0, :], ALU.subtract).then_inc(s_gap, 1)
                    return
                if k == 12:
                    ins = v.tensor_scalar(top[:, 0, :], top[:, 3, :], 1.0, None, ALU.add)
                if k == 13:
                    ins = v.reciprocal(top[:, 1, :], top[:, 0, :])
                if k == 14:
                    ins = v.tensor_tensor(top[:, 2, :], top[:, 3, :], top[:, 1, :], ALU.mult)
                if k == 15:
                    ins = v.tensor_tensor(pick[:, 0], pick[:, 0], over_e(top[:, 1, :]), ALU.mult)
                if k == 16:
                    ins = v.tensor_tensor(pick[:, 1], pick[:, 1], over_e(top[:, 2, :]), ALU.mult)
                if k == 17:
                    v.tensor_tensor(comb[:, bass.ds(im * (T * E), T * E)].rearrange("p (t e) -> p t e", e=E),
                                    pick[:, 0], pick[:, 1], ALU.add).then_inc(s_comb, 1)
                    return
                ins.then_inc(s_top, 1)

            def per_block(x):
                return x.unsqueeze(2).to_broadcast([128, NB, C])

            def step(g, c, has):
                lo, hi = norms(has)
                ybc = yb[:, c].rearrange("p (b c) -> p b c", b=NB)
                sl3, sl4 = SLOT2[prv(c, 3)], SLOT2[prv(c, 4)]
                ab = slice(0 if has(0) else 1, 2 if has(4) else 1)
                two = slice(0 if has(0) else 2, 3 if has(4) else 1, 2)
                if has(0):
                    wait(dve, s_ys, g + 1)
                    for b in range(NB):
                        last = v.bn_stats(st[:, 0, b, :], ybc[:, b, :])
                if has(4):
                    wait(dve, s_t2, g - 3)
                    for b in range(NB):
                        last = v.bn_stats(st[:, 1, b, :], t_s[:, sl4, b, :])
                if lo < hi:
                    last.then_inc(s_v, 1)
                    wait(dve, s_v, g * 4 + 1)
                    v.tensor_tensor(sm[:, 0, two, :], st[:, ab, :, 1], st[:, ab, :, 4], ALU.add)
                    v.tensor_tensor(sm[:, 1, two, :], st[:, ab, :, 1], st[:, ab, :, 4], ALU.subtract)
                    v.tensor_tensor(sm[:, 2, two, :], st[:, ab, :, 2], st[:, ab, :, 5], ALU.add).then_inc(s_v, 1)
                if has(3):
                    wait(dve, s_sq, g - 2)
                    v.tensor_reduce(sm[:, 0, 1, :], sq[:, :, 0:C], AX.X, ALU.add)
                    v.tensor_scalar(sm[:, 1, 1, :], sq[:, :, C], EPS_LN, None, ALU.mult)
                if lo < hi:
                    wait(dve, s_v, g * 4 + 2)
                    v.tensor_scalar(sm[:, 3, two, :], sm[:, 0, two, :], 0.5, None, ALU.mult)
                    v.tensor_tensor(sm[:, 4, two, :], sm[:, 1, two, :], sm[:, 1, two, :], ALU.mult).then_inc(s_v, 1)
                    wait(dve, s_v, g * 4 + 3)
                    v.scalar_tensor_tensor(sm[:, 4, two, :], sm[:, 4, two, :], C / 4.0, sm[:, 2, two, :], ALU.mult, ALU.add).then_inc(s_v, 1)
                if has(3):
                    v.scalar_tensor_tensor(sm[:, 5, 1, :], sm[:, 0, 1, :], 1.0 / C, sm[:, 1, 1, :], ALU.mult, ALU.add)
                if lo < hi:
                    wait(dve, s_v, g * 4 + 4)
                    v.tensor_scalar(sm[:, 5, two, :], sm[:, 4, two, :], 1.0 / C, EPS_LN, ALU.mult, ALU.add).then_inc(s_w, 1)
                im = route_image(g, c) if isinstance(g, int) else cur["period"] - (1 if c == 6 else 2)
                routed = None if im is None or c == 5 else 3 * ((c + 1) % 7)
                if routed is not None:
                    route(im, routed)
                    route(im, routed + 1)
                if lo < hi:
                    wait(dve, s_r, g + 1)
                    v.tensor_tensor(sm[:, 8, lo:hi, :], sm[:, 5, lo:hi, :], sm[:, 7, lo:hi, :], ALU.mult).then_inc(s_n, 1)
                    wait(dve, s_n, g * 3 + 1)
                    v.scalar_tensor_tensor(sm[:, 8, lo:hi, :], sm[:, 8, lo:hi, :], -0.5, sm[:, 7, lo:hi, :], ALU.mult, ALU.mult).then_inc(s_n, 1)
                    wait(dve, s_n, g * 3 + 2)
                    v.scalar_tensor_tensor(sm[:, 9, lo:hi, :], sm[:, 8, lo:hi, :], 1.5, sm[:, 7, lo:hi, :], ALU.add, ALU.mult).then_inc(s_n, 1)
                if has(0):
                    wait(dve, s_xnt, g)
                    v.tensor_tensor(xn_s[:, :, :], ybc, per_block(sm[:, 3, 0, :]), ALU.subtract).then_inc(s_xc, 1)
                if lo < hi:
                    wait(dve, s_n, g * 3 + 3)
                if has(3):
                    wait(dve, s_res, g - 4)
                    v.tensor_tensor(t_s[:, sl3], p7[:, 0:NB * (C + 1)].rearrange("p (b c) -> p b c", b=NB)[:, :, 0:C],
                                    per_block(sm[:, 9, 1, :]), ALU.mult).then_inc(s_t, 1)
                if has(0):
                    wait(dve, s_xc, g + 1)
                    v.tensor_tensor(xn_s[:, :, :], xn_s[:, :, :], per_block(sm[:, 9, 0, :]), ALU.mult).then_inc(s_xn, 1)
                if has(4):
                    wait(dve, s_res, g - 5)
                    wait(dve, s_tnt, g - 5)
                    v.tensor_tensor(tn_s[:, sl4], t_s[:, sl4], per_block(sm[:, 3, 2, :]), ALU.subtract).then_inc(s_tc, 1)
                if routed is not None:
                    route(im, routed + 2)
                if has(4):
                    wait(dve, s_tc, g - 3)
                    v.tensor_tensor(tn_s[:, sl4], tn_s[:, sl4], per_block(sm[:, 9, 2, :]), ALU.mult).then_inc(s_tn, 1)
                if has(6) and prv(c, 6) == 6:
                    wait(dve, s_ls, g - 5)
                    v.tensor_copy(pick[:, 2], logits[:, :, :]).then_inc(s_top, 1)

            cur = {}

            def walk_dve():
                for g in range(14):
                    step(g, g % 7, lambda d, g=g: d <= g)
                with dve.Fori(2, G // 7) as i:
                    cur["period"] = i
                    for c in range(7):
                        step(i * 7 + c, c, lambda d: True)
                for c in range(7):
                    step(G + c, c, lambda d, c=c: d > c)

            walk_dve()

            def ct_copy(g, c):
                wait(dve, s_ct, g + 1)
                v.tensor_copy(ct_s[0:H * CP, c, :], p7[0:H * CP, 0:CH]).then_inc(s_cts, 1)

            def low(g, c):
                wait(dve, s_hi, g + 1)
                v.tensor_tensor(thl[64:128, c], tdup[64:128, c].rearrange("p (h n) -> p h n", h=H),
                                thl[64:128, c].bitcast(f32), ALU.subtract).then_inc(s_lo, 1)

            def parts_step(g, c, k):
                src = comb[:, bass.ds(g * (NB * E), NB * E)].rearrange("p (b e) -> p b e", b=NB)
                parts = cparts[:, c].rearrange("p (b k e) -> p k b e", b=NB, k=CP // E)
                if k == 0:
                    wait(dve, s_ct, g - 1)
                    v.tensor_scalar(parts[:, 0], src, 1.0, None, ALU.mult).then_inc(s_cs, 1)
                else:
                    wait(dve, s_cs, g * 4 + k)
                if k == 1:
                    v.tensor_tensor(cr, src, parts[:, 0], ALU.subtract).then_inc(s_cs, 1)
                if k == 2:
                    v.tensor_copy(parts[:, 1], cr).then_inc(s_cs, 1)
                if k == 3:
                    v.tensor_tensor(cf, cr, parts[:, 1], ALU.subtract).then_inc(s_cs, 1)
                if k == 4:
                    v.tensor_copy(parts[:, 2], cf).then_inc(s_cpt, 1)

            def gate(g, c, j):
                u = g * 4 + j
                wait(dve, s_g, u + 1)
                wait(dve, s_c, u + 1)
                wait(dve, s_l2, u - 1)
                v.tensor_tensor(gated[:, j % 2, :].rearrange("p (h n) -> p h n", h=H),
                                hid[:, j % 2, :].rearrange("p (h n) -> p h n", h=H),
                                p01[:, :, 0:CH], ALU.mult).then_inc(s_gm, 1)

            def step3(g, c, has, more=True, routing=((), (), (), ())):
                if has(0):
                    for j in range(4):
                        if more and j < 2:
                            parts_step(g + 1, 1 - c, 2 * j)
                            parts_step(g + 1, 1 - c, 2 * j + 1)
                        if j == 2:
                            if more:
                                parts_step(g + 1, 1 - c, 4)
                            if has(1):
                                finish(g - 1, 1 - c)
                            if more:
                                low(g + 1, 1 - c)
                        if j == 3 and more:
                            ct_copy(g + 1, 1 - c)
                        gate(g, c, j)
                        for k in routing[j]:
                            route(NP - 1, k)
                elif has(1):
                    finish(g - 1, 1 - c)

            def finish(q, cq):
                wait(dve, s_tt, q + 1)
                stored(dve, q, cq)
                v.tensor_tensor(fin[:, cq, :], p7[:, 0:CH], resid[:, bass.ds(q * CH, CH)], ALU.add).then_inc(s_fin, 1)

            def stored(eng, q, cq):
                if isinstance(q, int):
                    wait(eng, s_out[cq], 32 * (q // 2))
                else:
                    wait(eng, s_out[cq], 32 * cur["fin"])

            low(0, 0)
            dve.wait_ge(s_comb, NP - 1)
            dve.wait_ge(s_zero, 3)
            for k in range(5):
                parts_step(0, 0, k)
            ct_copy(0, 0)
            for g in range(4):
                routing = {0: ((3, 4), (5, 6), (7, 8), (9, 10, 11)), 1: ((12, 13), (14, 15), (16,), (17,))}
                step3(g, g % 2, lambda d, g=g: d <= g, routing=routing.get(g, ((), (), (), ())))
            dve.wait_ge(s_comb, NP)
            with dve.Fori(2, G // 2 - 1) as i:
                cur["fin"] = i - 1
                step3(i * 2, 0, lambda d: True)
                cur["fin"] = i
                step3(i * 2 + 1, 1, lambda d: True)
            step3(G - 2, 0, lambda d: True)
            step3(G - 1, 1, lambda d: True, more=False)
            step3(G, 0, lambda d: d > 0, more=False)

        @blk.tensor
        def _(pe):
            t = nc.tensor
            for n in range(NP):
                pe.wait_ge(s_x1[n % 2], 16 * (n // 2 + 1))
                for k in range(PTOK):
                    hh = (n * PTOK + k) % 2
                    tile = x1[:, n % 2, k * C:(k + 1) * C]
                    last = t.matmul(p34[64 * hh:64 * hh + 64, 0, 0:C], tile, tile,
                                    start=(n * PTOK + k < 2), stop=(n * PTOK + k >= NP * PTOK - 2))
                last.then_inc(s_gram, 1)
            pe.wait_ge(s_const, 16 * 11)
            pe.wait_ge(s_zero, 1)
            pe.wait_ge(s_cd, 2)
            t.matmul(p2[:, 0:C], ones, colsum2[:, 0, :], start=True, stop=True)
            t.matmul(p2[:, C:C + 1], colsum2.rearrange("p a b -> p (a b)"), ones[:, 0:1], start=True, stop=True)
            t.matmul(p2[:, 2 * C:3 * C], fold, gram, start=True, stop=True).then_inc(s_cp, 1)
            pe.wait_ge(s_cd, 9)
            t.matmul(p7[0:64, 0:1], group, small1[0:64, 1:2], start=True, stop=True).then_inc(s_cp, 1)
            for it in range(ITERS - 1):
                pe.wait_ge(s_cd, 14 + 2 * it)
                t.matmul(p2[0:64, 0:2 * C], psig[0:64, 0, :], psig[0:64].rearrange("p a b -> p (a b)"),
                         start=True, stop=True).then_inc(s_cp, 1)
                pe.wait_ge(s_cd, 15 + 2 * it)
                t.matmul(p7[0:64, 0:C], pq[0:64, 0, :], pq[0:64, 1, :], start=True, stop=True).then_inc(s_cp, 1)
            pe.wait_ge(s_cd, 14 + 2 * (ITERS - 1) + 5)
            t.matmul(p2[:, 0:C], fold[0:64, :], rmat[0:64], start=True, stop=True).then_inc(s_cp, 1)
            pe.wait_ge(s_prep, 1)

            def flip(dst, src, weights, width=BLK, blocks=range(NB)):
                for b in blocks:
                    for h in range(H):
                        last = t.matmul(dst[64 * h:64 * h + 64, b * width:(b + 1) * width], src[:, b * BLK:(b + 1) * BLK],
                                        weights[:, h * width:(h + 1) * width], start=True, stop=True)
                return last

            def to_paired(dst, src):
                for b in range(NB // 2):
                    t.transpose(dst[:, b * 128:(b + 1) * 128], src[:, b * 128:(b + 1) * 128], eye[:, :])
                return flip(dst, src, eye, blocks=[NB - 1])

            def from_paired(dst, src, weights, width, bias=None):
                def product(region, stationary, moving, m):
                    if bias is not None:
                        t.matmul(region, ones_h[:, 0:m], bias[:, 0:m], start=True, stop=False)
                    return t.matmul(region, stationary, moving, start=bias is None, stop=True)

                for b in range(NB // 2):
                    product(dst[:, b * 2 * width:(b + 1) * 2 * width], src[:, b * 128:(b + 1) * 128], weights, 128)
                for h in range(H):
                    last = product(dst[64 * h:64 * h + 64, (NB - 1) * width:NB * width], src[:, (NB - 1) * BLK:CH],
                                   weights[:, h * width:(h + 1) * width], 64)
                return last

            def step(g, c, has):
                if has(0):
                    pe.wait_ge(s_x2[c], 32 * (g // 7 + 1) if isinstance(g, int) else 32 * (cur["i"] + 1))
                    wait(pe, s_tnts, g - 5)
                    to_paired(p01[:, 0], x2[:, SLOT3[c], :]).then_inc(s_xt, 1)
                if has(6):
                    q, sl = g - 6, SLOT2[prv(c, 6)]
                    wait(pe, s_tnts, q + 1)
                    wait(pe, s_xnts, min(g - 1, G) if isinstance(g, int) else g - 1)
                    wait(pe, s_ls, q)
                    from_paired(p2[:, CH:], tnt_s[:, sl, :], router[:, :, :].rearrange("p h e -> p (h e)"), E).then_inc(s_l, 1)
                if has(0):
                    wait(pe, s_ys, g)
                    wait(pe, s_xts, g + 1)
                    from_paired(p01[:, 1], xt_s[:, :], white[:, :, :].rearrange("p h c -> p (h c)"), C,
                                bias=bet0_rows).then_inc(s_y, 1)
                if has(1):
                    q = g - 1
                    wait(pe, s_xn, q + 1)
                    wait(pe, s_xnts, q)
                    wait(pe, s_ls, g - 5)
                    flip(p2, xn_s[:, :, :].rearrange("p b c -> p (b c)"), eye).then_inc(s_xnt, 1)
                if has(3):
                    q = g - 3
                    wait(pe, s_pm, q + 1)
                    wait(pe, s_vs, q + 1)
                    wait(pe, s_t, q)
                    for b in range(NB):
                        for h in range(H):
                            last = t.matmul(p7[64 * h:64 * h + 64, b * (C + 1):(b + 1) * (C + 1)],
                                            prob[:, b, 64 * h:64 * h + 64], v_s[:, b, h, :], start=True, stop=True)
                    last.then_inc(s_o, 1)
                if has(2):
                    q, cq = g - 2, prv(c, 2)
                    wait(pe, s_kts, q + 2 if has(1) else q + 1)
                    wait(pe, s_vs, q)
                    for b in range(NB):
                        last = t.transpose(p56[0:KEYS, b // 4, (b % 4) * 128:(b % 4 + 1) * 128],
                                           keys_t[:, cq, b * BLK:b * BLK + KEYS], eye[:, :])
                    last.then_inc(s_vt, 1)
                if has(5):
                    q, sl = g - 5, SLOT2[prv(c, 5)]
                    wait(pe, s_tn, q + 1)
                    if has(0):
                        wait(pe, s_xts, g + 1)
                    else:
                        wait(pe, s_tnts, q)
                    to_paired(p01[:, 0], tn_s[:, sl].rearrange("p b c -> p (b c)")).then_inc(s_tnt, 1)
                if has(2):
                    q, cq = g - 2, prv(c, 2)
                    wait(pe, s_xnts, q + 2 if has(1) else q + 1)
                    wait(pe, s_p, q)
                    for b in range(NB):
                        last = t.matmul(p34[0:KEYS, b // 4, (b % 4) * 128:(b % 4 + 1) * 128],
                                        keys_t[:, cq, b * BLK:b * BLK + KEYS], qry[:, SLOT2[cq], b, :],
                                        start=True, stop=True)
                    last.then_inc(s_s, 1)

            cur = {}
            for c in range(7):
                step(c, c, lambda d, c=c: d <= c)
            with pe.Fori(1, G // 7) as i:
                cur["i"] = i
                for c in range(7):
                    step(i * 7 + c, c, lambda d: True)
            for c in range(7):
                step(G + c, c, lambda d, c=c: d > c)

            pe.wait_ge(s_p, G)
            pe.wait_ge(s_vs, G)
            pe.wait_ge(s_t, G)
            pe.wait_ge(s_ls, G)
            pe.wait_ge(s_xnts, G)

            def comb_t(g, c):
                wait(pe, s_cpt, g + 1)
                wait(pe, s_fin, g - 1)
                for b in range(NB // 2):
                    t.matmul(p7[0:H * CP, b * 128:(b + 1) * 128], cparts[:, c, 2 * b * CP:2 * (b + 1) * CP], eye_h[:, :],
                             start=True, stop=True)
                for h in range(H):
                    last = t.matmul(p7[CP * h:CP * h + CP, (NB - 1) * BLK:CH], cparts[:, c, (NB - 1) * CP:NB * CP],
                                    eye_h[:, 64 * h:64 * h + 64], start=True, stop=True)
                last.then_inc(s_ct, 1)

            def first_layer(g, c, j):
                u = g * 4 + j
                bank = p34 if j % 2 == 0 else p56
                if j == 0:
                    wait(pe, s_lo, g + 1)
                wait(pe, s_g, u - 1)
                for k, w in enumerate((w1_hi, w1_lo)):
                    for h in range(H):
                        last = t.matmul(bank[:, h, 0:CH], w[:, 128 * j:128 * (j + 1)], thl[:, c, h, :],
                                        start=(k == 0), stop=(k == 1))
                last.then_inc(s_h, 1)

            def spread(g, c, j):
                u = g * 4 + j
                if j == 0:
                    wait(pe, s_cts, g + 1)
                wait(pe, s_gm, u)
                for h in range(H):
                    last = t.matmul(p01[:, h, 0:CH], selector[:, (4 * h + j) * 128:(4 * h + j + 1) * 128],
                                    ct_s[:, c, :], start=True, stop=True)
                last.then_inc(s_c, 1)

            def second_layer(g, c, j):
                u = g * 4 + j
                if j == 0:
                    wait(pe, s_y3s, g)
                    for p in range(PARTS):
                        for h in range(H):
                            t.matmul(p2[64 * h:64 * h + 64, 0:CH], b2_p[:, p, C * h:C * h + C], ct_s[:, c, :],
                                     start=(p == 0), stop=False)
                wait(pe, s_gm, u + 1)
                for h in range(H):
                    last = t.matmul(p2[64 * h:64 * h + 64, 0:CH], w2_s[:, j, :], gated[:, j % 2, h * CH:(h + 1) * CH],
                                    start=False, stop=(j == 3))
                last.then_inc(s_l2, 1)

            def back(g, more):
                wait(pe, s_y3s, g + 1)
                wait(pe, s_cts, g + 2 if more else g + 1)
                wait(pe, s_fin, g)
                to_paired(p7, y3).then_inc(s_tt, 1)

            def step3(g, c, has, more=True):
                for j in range(4):
                    if has(0):
                        first_layer(g, c, j)
                    if j == 3 and has(0) and more:
                        comb_t(g + 1, 1 - c)
                    if j < 2:
                        if has(1):
                            second_layer(g - 1, 1 - c, j + 2)
                    else:
                        if j == 2 and has(1):
                            back(g - 1, has(0))
                        if has(0):
                            second_layer(g, c, j - 2)
                    if has(0):
                        spread(g, c, j)

            comb_t(0, 0)
            step3(0, 0, lambda d: d <= 0)
            step3(1, 1, lambda d: d <= 1)
            with pe.Fori(1, G // 2 - 1) as i:
                step3(i * 2, 0, lambda d: True)
                step3(i * 2 + 1, 1, lambda d: True)
            step3(G - 2, 0, lambda d: True)
            step3(G - 1, 1, lambda d: True, more=False)
            step3(G, 0, lambda d: d > 0, more=False)


_INS = ['x', 'L0_conv_gamma', 'L0_conv_beta', 'L1_attn_gamma', 'L1_attn_beta', 'L1_ffn_router_w', 'L1_ffn_w1',
        'L1_ffn_b1', 'L1_ffn_w2', 'L1_ffn_b2']


def _constants(n_tokens):
    import numpy as np
    f = np.float32
    eye64 = np.eye(C, dtype=f)
    grp = np.kron(np.eye(C // M_GROUP, dtype=f), np.ones((M_GROUP, M_GROUP), f))
    block = np.tile(grp * f((1.0 - EPS_W) / (n_tokens - 1.0)), (2, 1))
    k, q = np.arange(KEYS)[:, None], np.arange(BLK)[None, :]
    band = ((k - q >= 0) & (k - q <= 2 * WIN)).astype(f)
    sel = np.zeros((128, H, 4, 2, C), f)
    for h in range(H):
        for p in range(PARTS):
            for e in range(E):
                sel[CP * h + E * p + e, h, e // 2, e % 2, :] = 1.0
    return {"eye": np.eye(128, dtype=f), "fold": np.tile(eye64, (2, 2)), "group": grp, "block": block,
            "band": band, "rank": np.arange(E, 0, -1).astype(f), "sel": sel.reshape(128, -1)}


def kernel(**inputs):
    import numpy as _np
    import concourse.bacc as _bacc
    from concourse import mybir as _mybir
    from concourse.bass_utils import run_bass_kernel_spmd as _run

    nc = _bacc.Bacc("TRN2", target_bir_lowering=False, num_devices=1)
    arrays, args = {}, []
    shape = inputs['x'].shape
    named = {n: inputs[n] for n in _INS}
    named.update({f"k_{n}": a for n, a in _constants(shape[0] * shape[1] * shape[2]).items()})
    for name, a in named.items():
        a = _np.ascontiguousarray(a)
        arrays[f"in_{name}_dram"] = a
        args.append(nc.dram_tensor(f"in_{name}_dram", a.shape, _mybir.dt.from_np(a.dtype), kind="ExternalInput").ap())
    args.append(nc.dram_tensor("out_0_dram", shape, _mybir.dt.float32, kind="ExternalOutput").ap())
    hybrid_kernel(nc, *args)
    r = _run(nc, [arrays], core_ids=[0])
    return r.results[0]["out_0_dram"]
```

```python
import concourse.bass as bass
from concourse import mybir
from contextlib import ExitStack

H = 2
BLK = 64
NB = 7
CH = NB * BLK
C = 64
WIN = 16
KEYS = BLK + 2 * WIN
E = 8
PARTS = 3
CP = 32
M_GROUP = 16
ITERS = 5
EPS_W = 1e-5
EPS_LN = 1e-5
SLOT2 = [0, 1, 0, 1, 0, 1, 2]
SLOT3 = [0, 1, 2, 0, 1, 2, 3]
NX = 4
ROUTE_GEXP = 3


def hybrid_kernel(nc, x, g0, b0, g1, b1v, rw, w1, b1, w2, b2, k_eye, k_fold, k_group, k_block, k_band,
                  k_rank, k_sel, out):
    f32, bf16, f32r = mybir.dt.float32, mybir.dt.bfloat16, mybir.dt.float32r
    ALU, ACT, AX = mybir.AluOpType, mybir.ActivationFunctionType, mybir.AxisListType
    IMGS, HH, WW, _ = x.shape
    NP = IMGS // H
    TOK = HH * WW
    CPI = TOK // CH
    G = NP * CPI
    N = IMGS * TOK
    PTOK = H * TOK // 128
    assert CPI == 7 and G % 2 == 0 and NP >= NX and PTOK * 128 == H * TOK
    SCALE = float(C) ** -0.5
    CUT = 2 * C * (PTOK // 8)
    PIECES = [(0, CUT), (CUT, 2 * CUT), (2 * CUT, 3 * CUT), (3 * CUT, PTOK * C)]

    x_flat = x.rearrange("i a b c -> (i a b c)")
    x_pairs = x_flat.rearrange("(n p f) -> n p f", n=NP, p=128)
    x_chunks = x_flat.rearrange("(h g b p c) -> h g p b c", h=H, g=G, b=NB, p=BLK)
    out_chunks = out.rearrange("i a b c -> (i a b c)").rearrange("(h g b p c) -> h g p b c", h=H, g=G, b=NB, p=BLK)
    spill = nc.dram_tensor("tn_spill", (G, 128, CH), f32).ap()

    ctx = ExitStack()
    with ctx:
        def sb(name, shape, dt=f32):
            return ctx.enter_context(nc.sbuf_tensor(name, shape, dt))

        def pb(name, shape):
            return ctx.enter_context(nc.psum_tensor(name, shape, f32))

        def sem(name):
            return ctx.enter_context(nc.semaphore(name))

        resid = sb("resid", [128, G * CH])
        comb = sb("comb", [128, G * NB * E])
        eye = sb("eye", [128, 128])
        band = sb("band", [KEYS, BLK])
        rank = sb("rank", [128, E])
        selector = sb("selector", [128, H * 4 * 128], bf16)
        eye_h = sb("eye_h", [128, 128], bf16)
        gam1 = sb("gam1", [128, C])
        bet1 = sb("bet1", [128, C])
        white = sb("white", [128, H, C])
        router = sb("router", [128, H, E])
        neg_mean = sb("neg_mean", [128, 1])
        w1_hi = sb("w1_hi", [128, E * C], f32r)
        w1_lo = sb("w1_lo", [128, E * C], f32r)
        w2_s = sb("w2_s", [128, 4, C])
        b1_s = sb("b1_s", [128, 4])
        b2_p = sb("b2_p", [128, 2, H * C], bf16)
        bet0_rows = sb("bet0_rows", [128, H * C], bf16)
        ones_h = sb("ones_h", [128, 128], bf16)
        ARENA = 9016
        arena = sb("arena", [128, ARENA])
        logits = sb("logits", [128, NB * CPI, E])

        def carve(at, shape, dt=f32, rows=128, base=arena, size=ARENA):
            n = 1
            for d in shape:
                n *= d
            cols = n if dt != bf16 else (n + 1) // 2
            assert at[0] + cols <= size, (at, n)
            view = base[0:rows, at[0]:at[0] + cols]
            at[0] += cols
            if dt != f32:
                view = view.bitcast(dt)
            if len(shape) == 2:
                view = view.rearrange("p (a b) -> p a b", a=shape[0])
            if len(shape) == 3:
                view = view.rearrange("p (a b c) -> p a b c", a=shape[0], b=shape[1])
            return view

        x1 = carve([0], [NX, PTOK * C], base=resid, size=G * CH)
        at = [4 * CH]

        colsum = carve(at, [NP, C])
        colsum2 = carve(at, [2, C])
        gram = carve(at, [C])
        srow = carve(at, [C])
        scol = carve(at, [1])
        outer = carve(at, [C])
        psig = carve(at, [2, C])
        pq = carve(at, [2, C])
        p15 = carve(at, [C])
        covd = carve(at, [C])
        small1 = carve(at, [16])
        rmat = carve(at, [C])
        sel_f = carve(at, [H * 4 * 128])
        w1_f = carve(at, [E * C])
        bias_f = carve(at, [(H + 1) * C])
        bias_p = carve(at, [PARTS, (H + 1) * C], bf16)
        fold = carve(at, [128])
        ones = carve(at, [128])
        group = carve(at, [64], rows=64)
        block = carve(at, [64])
        gam0 = carve(at, [C], rows=64)
        at = [0]
        x2 = carve(at, [4, CH])
        keys_t = carve(at, [7, CH + 2 * WIN])
        qry = carve(at, [3, NB, H * BLK])
        at = [ARENA - 3 * NB * CPI * E]
        pick = carve(at, [3, NB * CPI * E]).rearrange("p k (t e) -> p k t e", e=E)
        at3 = [0]
        tn_in = carve(at3, [2, H * CH], rows=64)
        hid = carve(at3, [2, H * CH])
        gated = carve(at3, [2, H * CH])
        y3 = carve(at3, [CH])
        fin = carve(at3, [2, CH])
        ct_s = carve(at3, [2, CH], bf16)
        cf = carve(at3, [NB, E])
        cr = carve(at3, [NB, E])
        cparts = carve(at3, [2, NB * CP], bf16)

        with nc.sbuf_tensor("yb", [128, CPI, CH], f32) as yb:
            pass
        thl = sb("thl", [128, 2, H, CH], f32r)
        sb("yb_tail", [128, (CPI - 2 * H) * CH])
        xt_s = sb("xt_s", [128, CH])
        xn_s = sb("xn_s", [128, NB, C])
        v_s = sb("v_s", [KEYS, NB, H, C + 1])
        prob = sb("prob", [KEYS, NB, H * BLK])
        sq = sb("sq", [128, NB, C + 1])
        t_s = sb("t_s", [128, 3, NB, C])
        tn_s = sb("tn_s", [128, 3, NB, C])
        tnt_s = sb("tnt_s", [128, 3, CH])
        st = sb("st", [128, 2, NB, 6])
        sm = sb("sm", [128, 10, 3, NB])
        top = sb("top", [128, 5, NB * CPI])

        p01 = pb("p01", [128, 2, 512])
        p2 = pb("p2", [128, 512])
        p34 = pb("p34", [128, 2, 512])
        p56 = pb("p56", [128, 2, 512])
        p7 = pb("p7", [128, 512])

        s_const, s_weights, s_x1 = sem("consts_in"), sem("weights_in"), [sem(f"x1_in{i}") for i in range(NX)]
        s_x1p = {n: [sem(f"x1_piece_in{n}_{i}") for i in range(3)] for n in (0, NP - 1)}
        s_zero, s_prep, s_prep_pool = sem("zeroed"), sem("prep_done"), sem("prep_pool")
        s_gram, s_colsum = sem("gram_done"), sem("colsum_done")
        s_cd, s_cp, s_ca = sem("chain_dve"), sem("chain_pe"), sem("chain_act")
        s_x2 = [sem(f"x2_in{i}") for i in range(7)]
        s_xt, s_xts, s_y, s_ys, s_yb = sem("xt"), sem("xt_copied"), sem("y"), sem("y_copied"), sem("yb")
        s_v, s_w, s_ln, s_r, s_n = sem("norm_steps"), sem("norm_var"), sem("norm_log"), sem("norm_rsqrt"), sem("norm_newton")
        s_xc, s_xn = sem("y_centred"), sem("xn")
        s_xnt, s_kts, s_xnts = sem("xn_t"), sem("keys_copied"), sem("keys_and_queries_copied")
        s_vt, s_vs, s_s, s_p, s_pm, s_o = sem("v"), sem("v_copied"), sem("scores"), sem("probs"), sem("probs_masked"), sem("pv")
        s_sq, s_t = sem("pv_squared"), sem("t_scaled")
        s_tp, s_t2 = sem("t_gamma"), sem("t2")
        s_tc, s_tn = sem("t_centred"), sem("tn")
        s_res, s_tnt, s_tnts, s_l, s_ls = sem("resid"), sem("tn_t"), sem("tn_t_copied"), sem("logits"), sem("logits_copied")
        s_sp = [sem(f"spilled{i}") for i in range(3)]
        s_top, s_gap, s_gexp, s_comb = sem("top_steps"), sem("top_gap"), sem("top_exp"), sem("combined")
        s_ti = [sem(f"tn_in{i}") for i in range(2)]
        s_hi, s_lo, s_cs, s_cpt = sem("tn_hi"), sem("tn_lo"), sem("comb_steps"), sem("comb_parts")
        s_ct, s_cts, s_ctd = sem("comb_t"), sem("comb_t_copied"), sem("comb_t_doubled")
        s_h, s_g, s_c, s_gm = sem("hidden"), sem("gelu"), sem("weights_spread"), sem("gated")
        s_l2, s_y3s, s_tt, s_fin = sem("second_layer"), sem("expert_sum_copied"), sem("back_t"), sem("fin")
        s_out = [sem(f"stored{i}") for i in range(2)]

        def wait(eng, s, n):
            if not isinstance(n, int) or n > 0:
                eng.wait_ge(s, n)

        def walk(eng, step, period, chunks, skew, after=lambda c: None):
            assert chunks % period == 0 and skew <= period
            for c in range(period):
                step(c, c, lambda d, c=c: d <= c)
            with eng.Fori(1, chunks // period) as i:
                for c in range(period):
                    step(i * period + c, c, lambda d: True)
            for c in range(skew):
                step(chunks + c, c, lambda d, c=c: d > c)
                after(c)

        def prv(c, d):
            return (c - d) % CPI

        def norms(has):
            lo = 0 if has(0) else 1 if has(3) else 2
            hi = 3 if has(4) else 2 if has(3) else 1
            return lo, hi

        def route_image(g, c):
            im = g // 7 - (1 if c == 6 else 2)
            return im if 0 <= im < NP - 1 and c != 5 else None

        blk = ctx.enter_context(nc.Block())

        @blk.sync
        def _(sp):
            def load(n):
                pieces = PIECES if n in s_x1p else [(0, PTOK * C)]
                for k, (lo, hi) in enumerate(pieces):
                    sp.dma_start(x1[:, n % NX, lo:hi], x_pairs[n][:, lo:hi])\
                      .then_inc(s_x1[n % NX] if k == len(pieces) - 1 else s_x1p[n][k], 16)

            for n in range(NX):
                load(n)
            for dst, src in ((eye[:, :], k_eye), (fold, k_fold), (group, k_group),
                             (block, k_block), (band[:, :], k_band),
                             (rank[:, :], k_rank.partition_broadcast(128)), (sel_f[:, :], k_sel),
                             (gam0, g0.rearrange("a b c d -> (a b c d)").partition_broadcast(64)),
                             (bias_f[:, H * C:], b0.rearrange("a b c d -> (a b c d)").partition_broadcast(128)),
                             (gam1[:, :], g1.partition_broadcast(128)),
                             (bet1[:, :], b1v.partition_broadcast(128))):
                sp.dma_start(dst, src).then_inc(s_const, 16)
            for n in range(NX, NP):
                sp.wait_ge(s_gram, n + 1 - NX)
                sp.wait_ge(s_colsum, n + 1 - NX)
                load(n)

            def step(g, c, has):
                if has(0):
                    wait(sp, s_xt, g - 2)
                    for h in range(H):
                        sp.dma_start(x2[64 * h:64 * h + 64, SLOT3[c], :].rearrange("p (b c) -> p b c", b=NB),
                                     x_chunks[h, g]).then_inc(s_x2[c], 16)

            walk(sp, step, 7, G, 0)

            sp.wait_ge(s_xt, G)

            def step3(g, c, has):
                if has(0):
                    wait(sp, s_hi, g - 1)
                    wait(sp, s_lo, g - 1)
                    sp.dma_start(tn_in[:, c, :].rearrange("p (h n) -> p h n", h=H),
                                 spill[g].rearrange("(h p) n -> p h n", h=H)).then_inc(s_ti[c], 16)
                if has(2):
                    wait(sp, s_fin, g - 1)
                    for h in range(H):
                        sp.dma_start(out_chunks[h, g - 2], fin[64 * h:64 * h + 64, c, :].rearrange("p (b c) -> p b c", b=NB))\
                          .then_inc(s_out[c], 16)

            for c in range(2):
                sp.wait_ge(s_sp[c], 16)
                step3(c, c, lambda d: d == 0)
            for k in range(3):
                spilled = sum(1 for c in range(7) if SLOT2[c] == k) * NP
                sp.wait_ge(s_sp[k], 16 * spilled)
            sp.wait_ge(s_s, G)
            with sp.Fori(1, G // 2) as i:
                for c in range(2):
                    step3(i * 2 + c, c, lambda d: True)
            for c in range(2):
                step3(G + c, c, lambda d: d > 0)
            for c in range(2):
                sp.wait_ge(s_out[c], 32 * (G // 2))

        @blk.gpsimd
        def _(pool):
            v = nc.gpsimd
            for dst, src in ((w1_f[0:64, :].rearrange("d (e f) -> d e f", e=E), w1.rearrange("e d f -> d e f")),
                             (w1_f[64:128, :].rearrange("d (e f) -> d e f", e=E), w1.rearrange("e d f -> d e f")),
                             (w2_s[:, :, :], w2.rearrange("(j e) f d -> (e f) j d", e=2)),
                             (b1_s[:, :], b1.rearrange("(j e) f -> (e f) j", e=2))):
                pool.dma_start(dst, src, allow_slow_non_contiguous=True).then_inc(s_weights, 16)
            v.memset(router[:, :, :], 0.0)
            v.memset(bias_f[:, 0:H * C], 0.0)
            v.memset(bet0_rows[:, :], 0.0)
            v.memset(b2_p[:, :, :], 0.0)
            v.memset(ones_h[:, :], 1.0)
            v.memset(white[:, :, :], 0.0)
            v.memset(ones, 1.0)
            v.memset(v_s[:, :, :, :], 1.0).then_inc(s_zero, 1)
            pool.wait_ge(s_zero, 1)
            for h in range(H):
                pool.dma_start(router[64 * h:64 * h + 64, h, :], rw.rearrange("e c -> c e"),
                               allow_slow_non_contiguous=True).then_inc(s_weights, 16)
                for d in range(2):
                    for p in range(PARTS):
                        r = H * CP * d + CP * h + E * p
                        pool.dma_start(bias_f[r:r + E, C * h:C * h + C], b2).then_inc(s_weights, 16)
            pool.wait_ge(s_weights, 16 * (4 + H * (1 + 2 * PARTS)))
            pool.wait_ge(s_const, 16 * 11)
            n = 0
            v.tensor_copy(selector[:, :], sel_f)
            v.tensor_copy(eye_h[:, :], eye[:, :])
            for p in range(PARTS):
                v.tensor_copy(bias_p[:, p, :], bias_f).then_inc(s_prep_pool, 1)
                n += 1
                pool.wait_ge(s_prep_pool, n)
                if p < PARTS - 1:
                    v.tensor_tensor(bias_f, bias_f, bias_p[:, p, :], ALU.subtract).then_inc(s_prep_pool, 1)
                    n += 1
                    pool.wait_ge(s_prep_pool, n)
            for p, (r, k) in enumerate(((0, 0), (64, 0), (0, 1))):
                v.tensor_copy(b2_p[r:r + 64, k, :], bias_p[r:r + 64, p, 0:H * C]).then_inc(s_prep_pool, 1)
                n += 1
                pool.wait_ge(s_prep_pool, n)
            for p in range(PARTS):
                r = slice(32 * p, 32 * p + 1)
                v.tensor_copy(bet0_rows[r, :].rearrange("p (b c) -> p b c", b=2),
                              bias_p[r, p, H * C:].unsqueeze(1).to_broadcast([1, 2, C])).then_inc(s_prep_pool, 1)
                n += 1
                pool.wait_ge(s_prep_pool, n)

            pool.wait_ge(s_prep, 1)
            v.memset(qry, 0.0)
            v.memset(keys_t[:, 0, 0:WIN], 0.0)
            v.memset(keys_t[:, 6, WIN + CH:], 0.0).then_inc(s_zero, 1)

            def step(g, c, has):
                if has(5):
                    q, sl = g - 5, SLOT2[prv(c, 5)]
                    wait(pool, s_tn, q + 1)
                    v.tensor_tensor(resid[:, bass.ds(q * CH, CH)], t_s[:, sl].rearrange("p b c -> p (b c)"),
                                    tn_s[:, sl].rearrange("p b c -> p (b c)"), ALU.add).then_inc(s_res, 1)
                if has(2):
                    q = g - 2
                    wait(pool, s_p, q + 1)
                    pv = prob[:, :, :].rearrange("p b (h q) -> p (b h) q", h=H)
                    v.tensor_tensor(pv, pv, band[:, :].unsqueeze(1).to_broadcast([KEYS, H * NB, BLK]),
                                    ALU.mult).then_inc(s_pm, 1)
                if has(3):
                    q, cq = g - 3, prv(c, 3)
                    sl = SLOT2[cq]
                    wait(pool, s_t, q + 1)
                    v.tensor_tensor(t_s[:, sl], t_s[:, sl], gam1[:, :].unsqueeze(1).to_broadcast([128, NB, C]),
                                    ALU.mult).then_inc(s_tp, 1)
                    wait(pool, s_tp, q + 1)
                    wait(pool, s_yb, q + 1)
                    v.tensor_tensor(t_s[:, sl], t_s[:, sl], yb[:, cq].rearrange("p (b c) -> p b c", b=NB),
                                    ALU.add).then_inc(s_t2, 1)
                if has(0):
                    wait(pool, s_xc, g + 1)
                    ybc = yb[:, c].rearrange("p (b c) -> p b c", b=NB)
                    v.tensor_tensor(ybc, ybc, bet1[:, :].unsqueeze(1).to_broadcast([128, NB, C]), ALU.add).then_inc(s_yb, 1)

            def after(c):
                if c == 2:
                    pool.wait_ge(s_s, G)
                    v.memset(ct_s, 0.0)
                    v.memset(cparts, 0.0).then_inc(s_zero, 1)

            walk(pool, step, 7, G, 5, after)

        @blk.scalar
        def _(act):
            a = nc.scalar
            a.preload_act_table_set("natural_log_exp_and_others")
            act.wait_ge(s_weights, 16 * (4 + H * (1 + 2 * PARTS)))
            a.activation(w1_hi[:, :], w1_f, ACT.Copy).then_inc(s_ca, 1)
            act.wait_ge(s_cd, 10)
            a.activation(small1[0:64, 3:4], small1[0:64, 0:1], ACT.Ln).then_inc(s_ca, 1)
            act.wait_ge(s_ca, 2)
            a.activation(small1[0:64, 4:5], small1[0:64, 3:4], ACT.Exp, scale=-0.5).then_inc(s_ca, 1)

            act.wait_ge(s_cd, 4)

            def step(g, c, has):
                if has(0):
                    wait(act, s_xt, g + 1)
                    wait(act, s_y, g)
                    a.activation(xt_s[:, :], p01[:, 0, 0:CH], ACT.Identity, bias=neg_mean[:, :]).then_inc(s_xts, 1)
                if has(6):
                    q, cq = g - 6, prv(c, 6)
                    wait(act, s_l, q + 1)
                    if cq == 0:
                        before = q // 7 - 1 if isinstance(q, int) else cur["period"] - 1
                        if not isinstance(before, int) or before >= 0:
                            wait(act, s_top, before * 17 + 1)
                    a.activation(logits[:, cq * NB:(cq + 1) * NB, :], p2[:, CH:CH + NB * E].rearrange("p (b e) -> p b e", b=NB),
                                 ACT.Copy).then_inc(s_ls, 1)
                if has(0):
                    wait(act, s_y, g + 1)
                    wait(act, s_t2, g - 6)
                    a.activation(yb[:, c, :], p01[:, 1, 0:CH], ACT.Copy).then_inc(s_ys, 1)
                if has(1):
                    q, cq = g - 1, prv(c, 1)
                    wait(act, s_xnt, q + 1)
                    wait(act, s_s, q - 1)
                    if isinstance(q, int) and q == 0:
                        act.wait_ge(s_zero, 2)
                    if cq < 6:
                        a.activation(keys_t[:, cq + 1, 0:WIN], p2[:, CH - WIN:CH], ACT.Copy)
                    if cq > 0:
                        a.activation(keys_t[:, cq - 1, WIN + CH:], p2[:, 0:WIN], ACT.Copy)
                    a.activation(keys_t[:, cq, WIN:WIN + CH], p2[:, 0:CH], ACT.Copy).then_inc(s_kts, 1)
                    for h in range(H):
                        r = slice(64 * h, 64 * h + 64)
                        last = a.activation(qry[r, SLOT2[cq], :, 64 * h:64 * h + 64], p2[r, 0:CH].rearrange("p (b q) -> p b q", b=NB), ACT.Copy)
                    last.then_inc(s_xnts, 1)
                if has(3):
                    q = g - 3
                    wait(act, s_o, q + 1)
                    wait(act, s_w, g)
                    a.activation(sq[:, :, :], p7[:, 0:NB * (C + 1)].rearrange("p (b c) -> p b c", b=NB),
                                 ACT.Square).then_inc(s_sq, 1)
                if has(2):
                    q = g - 2
                    wait(act, s_vt, q + 1)
                    wait(act, s_o, q)
                    a.activation(v_s[:, :, :, 0:C].rearrange("p b h c -> p (b h) c"),
                                 p56[0:KEYS].rearrange("p a (n c) -> p (a n) c", c=C)[:, 0:NB * H, :], ACT.Copy).then_inc(s_vs, 1)
                if has(5):
                    q, sl = g - 5, SLOT2[prv(c, 5)]
                    wait(act, s_tnt, q + 1)
                    wait(act, s_l, q - 1)
                    if not isinstance(q, int) or q >= 2:
                        uses = sum(1 for k in range(prv(c, 5)) if SLOT2[k] == sl)
                        per = sum(1 for k in range(7) if SLOT2[k] == sl)
                        image = q // 7 if isinstance(q, int) else cur["i"](prv(c, 5))
                        wait(act, s_sp[sl], 16 * (image * per + uses))
                    a.activation(tnt_s[:, sl, :], p01[:, 0, 0:CH], ACT.Copy).then_inc(s_tnts, 1)
                    wait(act, s_tnts, q + 1)
                    act.dma_start(spill[q], tnt_s[:, sl, :]).then_inc(s_sp[sl], 16)
                im = image_routed(g, c)
                if c == ROUTE_GEXP and im is not None:
                    wait(act, s_gap, im + 1)
                    a.activation(top[:, 3, :], top[:, 2, :], ACT.Exp).then_inc(s_gexp, 1)
                lo, hi = norms(has)
                if lo < hi:
                    wait(act, s_w, g + 1)
                    a.activation(sm[:, 6, lo:hi, :], sm[:, 5, lo:hi, :], ACT.Ln).then_inc(s_ln, 1)
                    wait(act, s_ln, g + 1)
                    a.activation(sm[:, 7, lo:hi, :], sm[:, 6, lo:hi, :], ACT.Exp, scale=-0.5).then_inc(s_r, 1)
                if has(2):
                    q = g - 2
                    wait(act, s_s, q + 1)
                    a.activation(prob[:, :, :].rearrange("p b q -> p (b q)"),
                                 p34[0:KEYS].rearrange("p a n -> p (a n)")[:, 0:NB * H * BLK], ACT.Exp, scale=SCALE).then_inc(s_p, 1)

            cur = {}

            def image_routed(g, c):
                return route_image(g, c) if isinstance(g, int) else cur["period"] - (1 if c == 6 else 2)

            for g in range(14):
                step(g, g % 7, lambda d, g=g: d <= g)
            with act.Fori(2, G // 7) as i:
                for c in range(7):
                    cur["i"] = lambda cq, c=c: i if cq <= c else i - 1
                    cur["period"] = i
                    step(i * 7 + c, c, lambda d: True)

            def gelu(g, c, j):
                u = g * 4 + j
                wait(act, s_h, u + 1)
                wait(act, s_gm, u - 1)
                a.activation(hid[:, j % 2, :].rearrange("p (h n) -> p h n", h=H),
                             (p34 if j % 2 == 0 else p56)[:, :, 0:CH], ACT.Gelu, bias=b1_s[:, j:j + 1]).then_inc(s_g, 1)

            def double(g, c):
                wait(act, s_cts, g + 1)
                wait(act, s_l2, 4 * (g - 1))
                a.activation(ct_s[H * CP:, c, :], ct_s[0:H * CP, c, :], ACT.Copy).then_inc(s_ctd, 1)

            def high(g, c, n):
                wait(act, s_ti[c], 16 * n)
                wait(act, s_h, 4 * (g - 1))
                a.activation(thl[0:64, c], tn_in[:, c].rearrange("p (h n) -> p h n", h=H), ACT.Copy).then_inc(s_hi, 1)

            def step3(g, c, has, i, first=0):
                if has(0):
                    for j in range(first, 2):
                        gelu(g, c, j)
                if has(1):
                    wait(act, s_l2, 4 * g)
                    wait(act, s_tt, g - 1)
                    a.activation(y3, p2[:, 0:CH], ACT.Copy).then_inc(s_y3s, 1)
                if has(0):
                    if not (isinstance(g, int) and g + 1 >= G):
                        high(g + 1, 1 - c, i + 1 + c)
                    gelu(g, c, 2)
                    gelu(g, c, 3)
                    if not (isinstance(g, int) and g + 1 >= G):
                        double(g + 1, 1 - c)

            for c in range(7):
                step(G + c, c, lambda d, c=c: d > c)
                if c == 3:
                    act.wait_ge(s_t2, G)
                    high(0, 0, 1)
                    a.preload_act_table_set("gelu_and_others")
                if c == 4:
                    act.wait_ge(s_zero, 3)
                    double(0, 0)
                if c == 5:
                    gelu(0, 0, 0)
            step3(0, 0, lambda d: d <= 0, 0, first=1)
            step3(1, 1, lambda d: d <= 1, 0)
            step3(2, 0, lambda d: True, 1)
            act.wait_ge(s_gap, NP)
            a.activation(top[:, 3, :], top[:, 2, :], ACT.Exp).then_inc(s_gexp, 1)
            step3(3, 1, lambda d: True, 1)
            with act.Fori(2, G // 2 - 1) as i:
                step3(i * 2, 0, lambda d: True, i)
                step3(i * 2 + 1, 1, lambda d: True, i)
            step3(G - 2, 0, lambda d: True, G // 2 - 1)
            step3(G - 1, 1, lambda d: True, G // 2 - 1)
            step3(G, 0, lambda d: d > 0, G // 2)

        @blk.vector
        def _(dve):
            v = nc.vector
            n_cd = [0]

            def link(ins):
                n_cd[0] += 1
                ins.then_inc(s_cd, 1)
                dve.wait_ge(s_cd, n_cd[0])

            for n in range(NP):
                if n in s_x1p:
                    for k in range(3):
                        dve.wait_ge(s_x1p[n][k], 16)
                dve.wait_ge(s_x1[n % NX], 16 * (n // NX + 1))
                v.tensor_reduce(colsum[:, n, :], x1[:, n % NX, :].rearrange("p (t c) -> p c t", c=C), AX.X, ALU.add).then_inc(s_colsum, 1)
            dve.wait_ge(s_colsum, NP)
            for k in range(2):
                last = v.tensor_reduce(colsum2[:, k, :], colsum.rearrange("p n c -> p c n"), AX.X, ALU.add)
            link(last)
            dve.wait_ge(s_ca, 1)
            v.tensor_tensor(w1_lo[:, :], w1_f, w1_hi[:, :].bitcast(f32), ALU.subtract)
            dve.wait_ge(s_gram, NP)
            v.tensor_copy(gram[0:64], p34[0:64, 0, 0:C])
            link(v.tensor_copy(gram[64:128], p34[64:128, 0, C:2 * C]))
            dve.wait_ge(s_cp, 1)
            v.tensor_copy(scol, p2[:, C:C + 1])
            link(v.tensor_copy(srow, p2[:, 0:C]))
            v.tensor_scalar(neg_mean[:, :], scol, -1.0 / N, None, ALU.mult)
            link(v.tensor_scalar(outer, srow, scol, -1.0 / N, ALU.mult, ALU.mult))
            link(v.tensor_tensor(outer, outer, p2[:, 2 * C:3 * C], ALU.add))
            link(v.tensor_tensor(outer, outer, block, ALU.mult))
            link(v.scalar_tensor_tensor(covd[0:64], eye[0:64, 0:64], EPS_W, outer[0:64], ALU.mult, ALU.add))
            link(v.tensor_tensor(p15[0:64], covd[0:64], eye[0:64, 0:64], ALU.mult))
            link(v.tensor_reduce(small1[0:64, 1:2], p15[0:64], AX.X, ALU.add))
            dve.wait_ge(s_cp, 2)
            link(v.tensor_copy(small1[0:64, 0:1], p7[0:64, 0:1]))
            link(v.reciprocal(small1[0:64, 2:3], small1[0:64, 0:1]))
            link(v.tensor_scalar(psig[0:64, 1, :], covd[0:64], small1[0:64, 2:3], None, ALU.mult))
            link(v.tensor_scalar(p15[0:64], eye[0:64, 0:64], 1.5, None, ALU.mult))
            link(v.scalar_tensor_tensor(psig[0:64, 0, :], psig[0:64, 1, :], -0.5, p15[0:64], ALU.mult, ALU.add))
            for it in range(ITERS - 1):
                dve.wait_ge(s_cp, 3 + 2 * it)
                v.tensor_scalar(p15[0:64], psig[0:64, 0, :], 1.5, None, ALU.mult)
                link(v.tensor_copy(pq[0:64].rearrange("p a b -> p (a b)"), p2[0:64, 0:2 * C]))
                dve.wait_ge(s_cp, 4 + 2 * it)
                link(v.scalar_tensor_tensor(psig[0:64, 0, :], p7[0:64, 0:C], -0.5, p15[0:64], ALU.mult, ALU.add))
            dve.wait_ge(s_ca, 3)
            link(v.tensor_tensor(small1[0:64, 5:6], small1[0:64, 0:1], small1[0:64, 4:5], ALU.mult))
            link(v.scalar_tensor_tensor(small1[0:64, 6:7], small1[0:64, 5:6], -0.5, small1[0:64, 4:5], ALU.mult, ALU.mult))
            link(v.scalar_tensor_tensor(small1[0:64, 7:8], small1[0:64, 6:7], 1.5, small1[0:64, 4:5], ALU.add, ALU.mult))
            link(v.tensor_scalar(rmat[0:64], psig[0:64, 0, :], small1[0:64, 7:8], None, ALU.mult))
            link(v.tensor_tensor(rmat[0:64], rmat[0:64], gam0, ALU.mult))
            dve.wait_ge(s_cp, 3 + 2 * (ITERS - 1))
            dve.wait_ge(s_zero, 1)
            v.tensor_copy(white[0:64, 0, :], p2[0:64, 0:C])
            dve.wait_ge(s_prep_pool, 4 * PARTS - 1)
            v.tensor_copy(white[64:128, 1, :], p2[64:128, 0:C]).then_inc(s_prep, 1)

            T = NB * CPI

            def route(im, k):
                if k == 12:
                    wait(dve, s_gexp, im + 1)
                else:
                    wait(dve, s_top, im * 17 + (k + 1 if k < 12 else k))
                val = pick[:, 2]
                r = 0 if k < 6 else 1

                def over_e(x):
                    return x.unsqueeze(2).to_broadcast([128, T, E])

                if k in (0, 6):
                    ins = v.tensor_reduce(top[:, r, :], val, AX.X, ALU.max)
                if k in (1, 7):
                    ins = v.tensor_tensor(pick[:, r], val, over_e(top[:, r, :]), ALU.is_equal)
                if k in (2, 8):
                    ins = v.tensor_tensor(pick[:, r], pick[:, r], rank[:, :].unsqueeze(1).to_broadcast([128, T, E]), ALU.mult)
                if k in (3, 9):
                    ins = v.tensor_reduce(top[:, 4, :], pick[:, r], AX.X, ALU.max)
                if k in (4, 10):
                    ins = v.tensor_tensor(pick[:, r], pick[:, r], over_e(top[:, 4, :]), ALU.is_equal)
                if k == 5:
                    ins = v.scalar_tensor_tensor(val, pick[:, 0], -1e30, val, ALU.mult, ALU.add)
                if k == 11:
                    v.tensor_tensor(top[:, 2, :], top[:, 1, :], top[:, 0, :], ALU.subtract).then_inc(s_gap, 1)
                    return
                if k == 12:
                    ins = v.tensor_scalar(top[:, 0, :], top[:, 3, :], 1.0, None, ALU.add)
                if k == 13:
                    ins = v.reciprocal(top[:, 1, :], top[:, 0, :])
                if k == 14:
                    ins = v.tensor_tensor(top[:, 2, :], top[:, 3, :], top[:, 1, :], ALU.mult)
                if k == 15:
                    ins = v.tensor_tensor(pick[:, 0], pick[:, 0], over_e(top[:, 1, :]), ALU.mult)
                if k == 16:
                    ins = v.tensor_tensor(pick[:, 1], pick[:, 1], over_e(top[:, 2, :]), ALU.mult)
                if k == 17:
                    v.tensor_tensor(comb[:, bass.ds(im * (T * E), T * E)].rearrange("p (t e) -> p t e", e=E),
                                    pick[:, 0], pick[:, 1], ALU.add).then_inc(s_comb, 1)
                    return
                ins.then_inc(s_top, 1)

            def per_block(x):
                return x.unsqueeze(2).to_broadcast([128, NB, C])

            def step(g, c, has):
                lo, hi = norms(has)
                ybc = yb[:, c].rearrange("p (b c) -> p b c", b=NB)
                sl3, sl4 = SLOT2[prv(c, 3)], SLOT2[prv(c, 4)]
                ab = slice(0 if has(0) else 1, 2 if has(4) else 1)
                two = slice(0 if has(0) else 2, 3 if has(4) else 1, 2)
                if has(0):
                    wait(dve, s_ys, g + 1)
                    for b in range(NB):
                        last = v.bn_stats(st[:, 0, b, :], ybc[:, b, :])
                if has(4):
                    wait(dve, s_t2, g - 3)
                    for b in range(NB):
                        last = v.bn_stats(st[:, 1, b, :], t_s[:, sl4, b, :])
                if lo < hi:
                    last.then_inc(s_v, 1)
                    wait(dve, s_v, g * 4 + 1)
                    v.tensor_tensor(sm[:, 0, two, :], st[:, ab, :, 1], st[:, ab, :, 4], ALU.add)
                    v.tensor_tensor(sm[:, 1, two, :], st[:, ab, :, 1], st[:, ab, :, 4], ALU.subtract)
                    v.tensor_tensor(sm[:, 2, two, :], st[:, ab, :, 2], st[:, ab, :, 5], ALU.add).then_inc(s_v, 1)
                if has(3):
                    wait(dve, s_sq, g - 2)
                    v.tensor_reduce(sm[:, 0, 1, :], sq[:, :, 0:C], AX.X, ALU.add)
                    v.tensor_scalar(sm[:, 1, 1, :], sq[:, :, C], EPS_LN, None, ALU.mult)
                if lo < hi:
                    wait(dve, s_v, g * 4 + 2)
                    v.tensor_scalar(sm[:, 3, two, :], sm[:, 0, two, :], 0.5, None, ALU.mult)
                    v.tensor_tensor(sm[:, 4, two, :], sm[:, 1, two, :], sm[:, 1, two, :], ALU.mult).then_inc(s_v, 1)
                    wait(dve, s_v, g * 4 + 3)
                    v.scalar_tensor_tensor(sm[:, 4, two, :], sm[:, 4, two, :], C / 4.0, sm[:, 2, two, :], ALU.mult, ALU.add).then_inc(s_v, 1)
                if has(3):
                    v.scalar_tensor_tensor(sm[:, 5, 1, :], sm[:, 0, 1, :], 1.0 / C, sm[:, 1, 1, :], ALU.mult, ALU.add)
                if lo < hi:
                    wait(dve, s_v, g * 4 + 4)
                    v.tensor_scalar(sm[:, 5, two, :], sm[:, 4, two, :], 1.0 / C, EPS_LN, ALU.mult, ALU.add).then_inc(s_w, 1)
                im = route_image(g, c) if isinstance(g, int) else cur["period"] - (1 if c == 6 else 2)
                routed = None if im is None or c == 5 else 3 * ((c + 1) % 7)
                if routed is not None:
                    route(im, routed)
                    route(im, routed + 1)
                if has(6) and prv(c, 6) == 6:
                    wait(dve, s_ls, g - 5)
                    v.tensor_copy(pick[:, 2], logits[:, :, :]).then_inc(s_top, 1)
                if lo < hi:
                    wait(dve, s_r, g + 1)
                    v.tensor_tensor(sm[:, 8, lo:hi, :], sm[:, 5, lo:hi, :], sm[:, 7, lo:hi, :], ALU.mult).then_inc(s_n, 1)
                    wait(dve, s_n, g * 3 + 1)
                    v.scalar_tensor_tensor(sm[:, 8, lo:hi, :], sm[:, 8, lo:hi, :], -0.5, sm[:, 7, lo:hi, :], ALU.mult, ALU.mult).then_inc(s_n, 1)
                    wait(dve, s_n, g * 3 + 2)
                    v.scalar_tensor_tensor(sm[:, 9, lo:hi, :], sm[:, 8, lo:hi, :], 1.5, sm[:, 7, lo:hi, :], ALU.add, ALU.mult).then_inc(s_n, 1)
                if has(0):
                    wait(dve, s_xnt, g)
                    v.tensor_tensor(xn_s[:, :, :], ybc, per_block(sm[:, 3, 0, :]), ALU.subtract).then_inc(s_xc, 1)
                if lo < hi:
                    wait(dve, s_n, g * 3 + 3)
                if has(3):
                    wait(dve, s_res, g - 4)
                    v.tensor_tensor(t_s[:, sl3], p7[:, 0:NB * (C + 1)].rearrange("p (b c) -> p b c", b=NB)[:, :, 0:C],
                                    per_block(sm[:, 9, 1, :]), ALU.mult).then_inc(s_t, 1)
                if has(0):
                    wait(dve, s_xc, g + 1)
                    v.tensor_tensor(xn_s[:, :, :], xn_s[:, :, :], per_block(sm[:, 9, 0, :]), ALU.mult).then_inc(s_xn, 1)
                if has(4):
                    wait(dve, s_res, g - 5)
                    wait(dve, s_tnt, g - 5)
                    v.tensor_tensor(tn_s[:, sl4], t_s[:, sl4], per_block(sm[:, 3, 2, :]), ALU.subtract).then_inc(s_tc, 1)
                if routed is not None:
                    route(im, routed + 2)
                if has(4):
                    wait(dve, s_tc, g - 3)
                    v.tensor_tensor(tn_s[:, sl4], tn_s[:, sl4], per_block(sm[:, 9, 2, :]), ALU.mult).then_inc(s_tn, 1)

            cur = {}

            for g in range(14):
                step(g, g % 7, lambda d, g=g: d <= g)
            with dve.Fori(2, G // 7) as i:
                cur["period"] = i
                for c in range(7):
                    step(i * 7 + c, c, lambda d: True)

            def ct_copy(g, c):
                wait(dve, s_ct, g + 1)
                v.tensor_copy(ct_s[0:H * CP, c, :], p7[0:H * CP, 0:CH]).then_inc(s_cts, 1)

            def low(g, c):
                wait(dve, s_hi, g + 1)
                v.tensor_tensor(thl[64:128, c], tn_in[:, c].rearrange("p (h n) -> p h n", h=H),
                                thl[0:64, c].bitcast(f32), ALU.subtract).then_inc(s_lo, 1)

            def parts_step(g, c, k):
                src = comb[:, bass.ds(g * (NB * E), NB * E)].rearrange("p (b e) -> p b e", b=NB)
                parts = cparts[:, c].rearrange("p (b k e) -> p k b e", b=NB, k=CP // E)
                if k == 0:
                    wait(dve, s_ct, g - 1)
                    v.tensor_scalar(parts[:, 0], src, 1.0, None, ALU.mult).then_inc(s_cs, 1)
                else:
                    wait(dve, s_cs, g * 4 + k)
                if k == 1:
                    v.tensor_tensor(cr, src, parts[:, 0], ALU.subtract).then_inc(s_cs, 1)
                if k == 2:
                    v.tensor_copy(parts[:, 1], cr).then_inc(s_cs, 1)
                if k == 3:
                    v.tensor_tensor(cf, cr, parts[:, 1], ALU.subtract).then_inc(s_cs, 1)
                if k == 4:
                    v.tensor_copy(parts[:, 2], cf).then_inc(s_cpt, 1)

            def gate(g, c, j):
                u = g * 4 + j
                wait(dve, s_g, u + 1)
                wait(dve, s_c, u + 1)
                wait(dve, s_l2, u - 1)
                v.tensor_tensor(gated[:, j % 2, :].rearrange("p (h n) -> p h n", h=H),
                                hid[:, j % 2, :].rearrange("p (h n) -> p h n", h=H),
                                p01[:, :, 0:CH], ALU.mult).then_inc(s_gm, 1)

            def step3(g, c, has, more=True, routing=((), (), (), ())):
                if has(0):
                    for j in range(4):
                        if more and j < 2:
                            parts_step(g + 1, 1 - c, 2 * j)
                            parts_step(g + 1, 1 - c, 2 * j + 1)
                        if j == 2:
                            if more:
                                parts_step(g + 1, 1 - c, 4)
                                low(g + 1, 1 - c)
                            if has(1):
                                finish(g - 1, 1 - c)
                        if j == 3 and more:
                            ct_copy(g + 1, 1 - c)
                        gate(g, c, j)
                        for k in routing[j]:
                            route(NP - 1, k)
                elif has(1):
                    finish(g - 1, 1 - c)

            def finish(q, cq):
                wait(dve, s_tt, q + 1)
                stored(dve, q, cq)
                v.tensor_tensor(fin[:, cq, :], p7[:, 0:CH], resid[:, bass.ds(q * CH, CH)], ALU.add).then_inc(s_fin, 1)

            def stored(eng, q, cq):
                if isinstance(q, int):
                    wait(eng, s_out[cq], 32 * (q // 2))
                else:
                    wait(eng, s_out[cq], 32 * cur["fin"])

            for c in range(7):
                if c == 4:
                    ct_copy(0, 0)
                step(G + c, c, lambda d, c=c: d > c)
                if c == 3:
                    dve.wait_ge(s_zero, 3)
                    dve.wait_ge(s_comb, NP - 2)
                    for k in range(5):
                        parts_step(0, 0, k)
                    low(0, 0)
            dve.wait_ge(s_comb, NP - 1)
            dve.wait_ge(s_res, G)
            for g in range(4):
                routing = [(4 * g + j,) for j in range(4)] if g < 3 else [(12, 13), (14, 15), (16,), (17,)]
                step3(g, g % 2, lambda d, g=g: d <= g, routing=routing)
            dve.wait_ge(s_comb, NP)
            with dve.Fori(2, G // 2 - 1) as i:
                cur["fin"] = i - 1
                step3(i * 2, 0, lambda d: True)
                cur["fin"] = i
                step3(i * 2 + 1, 1, lambda d: True)
            step3(G - 2, 0, lambda d: True)
            step3(G - 1, 1, lambda d: True, more=False)
            step3(G, 0, lambda d: d > 0, more=False)

        @blk.tensor
        def _(pe):
            t = nc.tensor
            def flip(dst, src, weights, width=BLK, blocks=range(NB)):
                for b in blocks:
                    for h in range(H):
                        last = t.matmul(dst[64 * h:64 * h + 64, b * width:(b + 1) * width], src[:, b * BLK:(b + 1) * BLK],
                                        weights[:, h * width:(h + 1) * width], start=True, stop=True)
                return last

            def to_paired(dst, src):
                for b in range(NB // 2):
                    t.transpose(dst[:, b * 128:(b + 1) * 128], src[:, b * 128:(b + 1) * 128], eye[:, :])
                return flip(dst, src, eye, blocks=[NB - 1])

            def from_paired(dst, src, weights, width, bias=None):
                def product(region, stationary, moving, m):
                    if bias is not None:
                        t.matmul(region, ones_h[:, 0:m], bias[:, 0:m], start=True, stop=False)
                    return t.matmul(region, stationary, moving, start=bias is None, stop=True)

                for b in range(NB // 2):
                    product(dst[:, b * 2 * width:(b + 1) * 2 * width], src[:, b * 128:(b + 1) * 128], weights, 128)
                for h in range(H):
                    last = product(dst[64 * h:64 * h + 64, (NB - 1) * width:NB * width], src[:, (NB - 1) * BLK:CH],
                                   weights[:, h * width:(h + 1) * width], 64)
                return last

            for m in range(NP // 2):
                two = x1[:, 2 * m % NX:2 * m % NX + 2, :].rearrange("p a f -> p (a f)")
                for k in range(PTOK):
                    for n in range(2 * m, 2 * m + 2):
                        lo, hi = k * 2 * C - (n - 2 * m) * PTOK * C, (k + 1) * 2 * C - (n - 2 * m) * PTOK * C
                        for p in range(3):
                            if n in s_x1p and lo <= PIECES[p][0] < hi:
                                pe.wait_ge(s_x1p[n][p], 16)
                        if lo <= (PIECES[3][0] if n in s_x1p else 0) < hi:
                            pe.wait_ge(s_x1[n % NX], 16 * (n // NX + 1))
                    tile = two[:, k * 2 * C:(k + 1) * 2 * C]
                    last = t.matmul(p34[:, 0, 0:2 * C], tile, tile, start=(m == 0 and k == 0),
                                    stop=(m == NP // 2 - 1 and k == PTOK - 1))
                    if k in (PTOK // 2, PTOK - 1):
                        last.then_inc(s_gram, 1)
            pe.wait_ge(s_const, 16 * 11)
            pe.wait_ge(s_zero, 1)
            pe.wait_ge(s_cd, 2)
            t.matmul(p2[:, 0:C], ones, colsum2[:, 0, :], start=True, stop=True)
            t.matmul(p2[:, C:C + 1], colsum2.rearrange("p a b -> p (a b)"), ones[:, 0:1], start=True, stop=True)
            t.matmul(p2[:, 2 * C:3 * C], fold, gram, start=True, stop=True).then_inc(s_cp, 1)
            pe.wait_ge(s_x2[0], 32)
            to_paired(p01[:, 0], x2[:, 0, :]).then_inc(s_xt, 1)
            pe.wait_ge(s_cd, 9)
            t.matmul(p7[0:64, 0:1], group, small1[0:64, 1:2], start=True, stop=True).then_inc(s_cp, 1)
            for it in range(ITERS - 1):
                pe.wait_ge(s_cd, 14 + 2 * it)
                t.matmul(p2[0:64, 0:2 * C], psig[0:64, 0, :], psig[0:64].rearrange("p a b -> p (a b)"),
                         start=True, stop=True).then_inc(s_cp, 1)
                pe.wait_ge(s_cd, 15 + 2 * it)
                t.matmul(p7[0:64, 0:C], pq[0:64, 0, :], pq[0:64, 1, :], start=True, stop=True).then_inc(s_cp, 1)
            pe.wait_ge(s_cd, 14 + 2 * (ITERS - 1) + 5)
            t.matmul(p2[:, 0:C], fold[0:64, :], rmat[0:64], start=True, stop=True).then_inc(s_cp, 1)

            def step(g, c, has):
                if has(0) and not (isinstance(g, int) and g == 0):
                    pe.wait_ge(s_x2[c], 32 * (g // 7 + 1) if isinstance(g, int) else 32 * (cur["i"] + 1))
                    wait(pe, s_tnts, g - 5)
                    to_paired(p01[:, 0], x2[:, SLOT3[c], :]).then_inc(s_xt, 1)
                if has(6):
                    q, sl = g - 6, SLOT2[prv(c, 6)]
                    wait(pe, s_tnts, q + 1)
                    wait(pe, s_xnts, min(g - 1, G) if isinstance(g, int) else g - 1)
                    wait(pe, s_ls, q)
                    from_paired(p2[:, CH:], tnt_s[:, sl, :], router[:, :, :].rearrange("p h e -> p (h e)"), E).then_inc(s_l, 1)
                if has(0):
                    if isinstance(g, int) and g == 0:
                        pe.wait_ge(s_prep, 1)
                    wait(pe, s_ys, g)
                    wait(pe, s_xts, g + 1)
                    from_paired(p01[:, 1], xt_s[:, :], white[:, :, :].rearrange("p h c -> p (h c)"), C,
                                bias=bet0_rows).then_inc(s_y, 1)
                if has(1):
                    q = g - 1
                    wait(pe, s_xn, q + 1)
                    wait(pe, s_xnts, q)
                    wait(pe, s_ls, g - 5)
                    flip(p2, xn_s[:, :, :].rearrange("p b c -> p (b c)"), eye).then_inc(s_xnt, 1)
                if has(3):
                    q = g - 3
                    wait(pe, s_pm, q + 1)
                    wait(pe, s_vs, q + 1)
                    wait(pe, s_t, q)
                    for b in range(NB):
                        for h in range(H):
                            last = t.matmul(p7[64 * h:64 * h + 64, b * (C + 1):(b + 1) * (C + 1)],
                                            prob[:, b, 64 * h:64 * h + 64], v_s[:, b, h, :], start=True, stop=True)
                    last.then_inc(s_o, 1)
                if has(2):
                    q, cq = g - 2, prv(c, 2)
                    wait(pe, s_kts, q + 2 if has(1) else q + 1)
                    wait(pe, s_vs, q)
                    for b in range(NB):
                        last = t.transpose(p56[0:KEYS, b // 4, (b % 4) * 128:(b % 4 + 1) * 128],
                                           keys_t[:, cq, b * BLK:b * BLK + KEYS], eye[:, :])
                    last.then_inc(s_vt, 1)
                if has(5):
                    q, sl = g - 5, SLOT2[prv(c, 5)]
                    wait(pe, s_tn, q + 1)
                    if has(0):
                        wait(pe, s_xts, g + 1)
                    else:
                        wait(pe, s_tnts, q)
                    to_paired(p01[:, 0], tn_s[:, sl].rearrange("p b c -> p (b c)")).then_inc(s_tnt, 1)
                if has(2):
                    q, cq = g - 2, prv(c, 2)
                    wait(pe, s_xnts, q + 2 if has(1) else q + 1)
                    wait(pe, s_p, q)
                    for b in range(NB):
                        last = t.matmul(p34[0:KEYS, b // 4, (b % 4) * 128:(b % 4 + 1) * 128],
                                        keys_t[:, cq, b * BLK:b * BLK + KEYS], qry[:, SLOT2[cq], b, :],
                                        start=True, stop=True)
                    last.then_inc(s_s, 1)

            cur = {}
            for c in range(7):
                step(c, c, lambda d, c=c: d <= c)
            with pe.Fori(1, G // 7) as i:
                cur["i"] = i
                for c in range(7):
                    step(i * 7 + c, c, lambda d: True)
            def comb_t(g, c):
                wait(pe, s_cpt, g + 1)
                wait(pe, s_fin, g - 1)
                for b in range(NB // 2):
                    t.matmul(p7[0:H * CP, b * 128:(b + 1) * 128], cparts[:, c, 2 * b * CP:2 * (b + 1) * CP], eye_h[:, :],
                             start=True, stop=True)
                for h in range(H):
                    last = t.matmul(p7[CP * h:CP * h + CP, (NB - 1) * BLK:CH], cparts[:, c, (NB - 1) * CP:NB * CP],
                                    eye_h[:, 64 * h:64 * h + 64], start=True, stop=True)
                last.then_inc(s_ct, 1)

            def first_layer(g, c, j):
                u = g * 4 + j
                bank = p34 if j % 2 == 0 else p56
                if j == 0:
                    wait(pe, s_lo, g + 1)
                wait(pe, s_g, u - 1)
                for k, w in enumerate((w1_hi, w1_lo)):
                    for h in range(H):
                        last = t.matmul(bank[:, h, 0:CH], w[:, 128 * j:128 * (j + 1)], thl[:, c, h, :],
                                        start=(k == 0), stop=(k == 1))
                last.then_inc(s_h, 1)

            def spread(g, c, j):
                u = g * 4 + j
                if j == 0:
                    wait(pe, s_ctd, g + 1)
                wait(pe, s_gm, u)
                for h in range(H):
                    last = t.matmul(p01[:, h, 0:CH], selector[:, (4 * h + j) * 128:(4 * h + j + 1) * 128],
                                    ct_s[:, c, :], start=True, stop=True)
                last.then_inc(s_c, 1)

            def second_layer(g, c, j):
                u = g * 4 + j
                if j == 0:
                    wait(pe, s_y3s, g)
                    for p in range(2):
                        for h in range(H):
                            t.matmul(p2[64 * h:64 * h + 64, 0:CH], b2_p[:, p, C * h:C * h + C], ct_s[:, c, :],
                                     start=(p == 0), stop=False)
                wait(pe, s_gm, u + 1)
                for h in range(H):
                    last = t.matmul(p2[64 * h:64 * h + 64, 0:CH], w2_s[:, j, :], gated[:, j % 2, h * CH:(h + 1) * CH],
                                    start=False, stop=(j == 3))
                last.then_inc(s_l2, 1)

            def back(g, more):
                wait(pe, s_y3s, g + 1)
                wait(pe, s_cts, g + 2 if more else g + 1)
                wait(pe, s_fin, g)
                to_paired(p7, y3).then_inc(s_tt, 1)

            def step3(g, c, has, more=True, first=0):
                for j in range(4):
                    if has(0) and j >= first:
                        first_layer(g, c, j)
                    if j == 3 and has(0) and more:
                        comb_t(g + 1, 1 - c)
                    if j < 2:
                        if has(1):
                            second_layer(g - 1, 1 - c, j + 2)
                    else:
                        if j == 2 and has(1):
                            back(g - 1, has(0))
                        if has(0):
                            second_layer(g, c, j - 2)
                    if has(0):
                        spread(g, c, j)

            for c in range(7):
                step(G + c, c, lambda d, c=c: d > c)
                if c == 4:
                    pe.wait_ge(s_t, G)
                    comb_t(0, 0)
                    pe.wait_ge(s_p, G)
                    first_layer(0, 0, 0)
                    pe.wait_ge(s_vs, G)
                    first_layer(0, 0, 1)
            pe.wait_ge(s_tnts, G)
            pe.wait_ge(s_ys, G)
            pe.wait_ge(s_ls, G)
            pe.wait_ge(s_xnts, G)
            step3(0, 0, lambda d: d <= 0, first=2)
            step3(1, 1, lambda d: d <= 1)
            with pe.Fori(1, G // 2 - 1) as i:
                step3(i * 2, 0, lambda d: True)
                step3(i * 2 + 1, 1, lambda d: True)
            step3(G - 2, 0, lambda d: True)
            step3(G - 1, 1, lambda d: True, more=False)
            step3(G, 0, lambda d: d > 0, more=False)


_INS = ['x', 'L0_conv_gamma', 'L0_conv_beta', 'L1_attn_gamma', 'L1_attn_beta', 'L1_ffn_router_w', 'L1_ffn_w1',
        'L1_ffn_b1', 'L1_ffn_w2', 'L1_ffn_b2']


def _constants(n_tokens):
    import numpy as np
    f = np.float32
    eye64 = np.eye(C, dtype=f)
    grp = np.kron(np.eye(C // M_GROUP, dtype=f), np.ones((M_GROUP, M_GROUP), f))
    block = np.tile(grp * f((1.0 - EPS_W) / (n_tokens - 1.0)), (2, 1))
    k, q = np.arange(KEYS)[:, None], np.arange(BLK)[None, :]
    band = ((k - q >= 0) & (k - q <= 2 * WIN)).astype(f)
    sel = np.zeros((128, H, 4, 2, C), f)
    for h in range(H):
        for p in range(PARTS):
            for e in range(E):
                sel[CP * h + E * p + e, h, e // 2, e % 2, :] = 1.0
    return {"eye": np.eye(128, dtype=f), "fold": np.tile(eye64, (2, 2)), "group": grp, "block": block,
            "band": band, "rank": np.arange(E, 0, -1).astype(f), "sel": sel.reshape(128, -1)}


def kernel(**inputs):
    import numpy as _np
    import concourse.bacc as _bacc
    from concourse import mybir as _mybir
    from concourse.bass_utils import run_bass_kernel_spmd as _run

    nc = _bacc.Bacc("TRN2", target_bir_lowering=False, num_devices=1)
    arrays, args = {}, []
    shape = inputs['x'].shape
    named = {n: inputs[n] for n in _INS}
    named.update({f"k_{n}": a for n, a in _constants(shape[0] * shape[1] * shape[2]).items()})
    for name, a in named.items():
        a = _np.ascontiguousarray(a)
        arrays[f"in_{name}_dram"] = a
        args.append(nc.dram_tensor(f"in_{name}_dram", a.shape, _mybir.dt.from_np(a.dtype), kind="ExternalInput").ap())
    args.append(nc.dram_tensor("out_0_dram", shape, _mybir.dt.float32, kind="ExternalOutput").ap())
    hybrid_kernel(nc, *args)
    r = _run(nc, [arrays], core_ids=[0])
    return r.results[0]["out_0_dram"]
```
